# Optimizing a Trainium2 kernel written in Bass

```python
import numpy as np
import jax
import jax.numpy as jnp

def _softmax(x, axis=-1):
    return jax.nn.softmax(x, axis=axis)

def _gelu(x):
    return jax.nn.gelu(x, approximate=True)

def _silu(x):
    return jax.nn.silu(x)

def _sigmoid(x):
    return jax.nn.sigmoid(x)

def _layernorm(x, axis=-1, eps=1e-05):
    m = jnp.mean(x, axis=axis, keepdims=True)
    v = jnp.var(x, axis=axis, keepdims=True)
    return (x - m) / jnp.sqrt(v + eps)

def _scatter_add(tgt, idx, src, axis=0):
    return tgt.at[idx].add(src)

def _segment_sum(src, seg, n):
    return jax.ops.segment_sum(src, seg, n)
kernel_name = 'mk_flamingo_gated_d2_seqx_r8_3b3645'

def setup_inputs(seed: int=0):
    np.random.seed(seed)
    _w = jnp.asarray

    def _rec_inputs():
        import jax
        import jax.numpy as jnp
        _rk = jax.random.key(seed)
        x = 0.0002279 + 0.9999 * jax.random.normal(jax.random.fold_in(_rk, 1), (16, 100, 128), jnp.float32)
        _lenS = 100 - jax.random.randint(jax.random.fold_in(_rk, 7), (16,), 0, max(1, 100 // 4) + 1, jnp.int32)
        _lenS2 = 1444 - jax.random.randint(jax.random.fold_in(_rk, 8), (16,), 0, max(1, 1444 // 4) + 1, jnp.int32)
        _ctx_1024P = jax.random.normal(jax.random.fold_in(_rk, 11), (16, 16, 128), jnp.float32)
        _ctx_1024c = jax.random.dirichlet(jax.random.fold_in(_rk, 511), 0.3 * jnp.ones((16,), jnp.float32), (16, 1444))
        _ctx_1024t = jnp.einsum('bsk,bkd->bsd', _ctx_1024c, _ctx_1024P)
        _ctx_1024t = _ctx_1024t * jax.lax.rsqrt(jnp.mean(jnp.square(_ctx_1024t)) + 1e-12) * 0.953939
        ctx_1024 = -0.000125008 + 0.999885 * (_ctx_1024t + 0.3 * jax.random.normal(jax.random.fold_in(_rk, 611), (16, 1444, 128), jnp.float32))
        _g = jax.random.normal(jax.random.fold_in(_rk, 9001), (2, 2), jnp.float32)
        _g = jnp.sign(_g) * jnp.maximum(jnp.abs(_g), 1.0) + (_g == 0) * 1.0
        g_xattn = _g[0]
        g_ffn = _g[1]
        return (x, ctx_1024, g_xattn, g_ffn)
    x, ctx_1024, g_xattn, g_ffn = _rec_inputs()

    def _L0_xattn_setup():
        import jax, jax.numpy as jnp
        import numpy as np
        DIM = 128
        HEADS = 8
        DIM_HEAD = 64
        INNER = HEADS * DIM_HEAD
        EPS = 1e-05

        def layernorm(x, w, b):
            mu = jnp.mean(x, axis=-1, keepdims=True)
            var = jnp.var(x, axis=-1, keepdims=True)
            return (x - mu) * jax.lax.rsqrt(var + EPS) * w + b
        key = jax.random.key(seed)
        ks = jax.random.split(key, 7)
        b, n_media, n_lat = (16, 256, 64)
        x = jax.random.normal(ks[0], (b, n_media, DIM), dtype=jnp.float32)
        latents = jax.random.normal(ks[1], (b, n_lat, DIM), dtype=jnp.float32)
        ln_m_w = jnp.ones((DIM,), jnp.float32)
        ln_m_b = jnp.zeros((DIM,), jnp.float32)
        ln_l_w = jnp.ones((DIM,), jnp.float32)
        ln_l_b = jnp.zeros((DIM,), jnp.float32)
        Wq = jax.random.normal(ks[2], (DIM, INNER), dtype=jnp.float32) * DIM ** (-0.5)
        Wkv = jax.random.normal(ks[3], (DIM, 2 * INNER), dtype=jnp.float32) * DIM ** (-0.5)
        Wout = jax.random.normal(ks[4], (INNER, DIM), dtype=jnp.float32) * INNER ** (-0.5)
        return {'x': x, 'latents': latents, 'ln_m_w': ln_m_w, 'ln_m_b': ln_m_b, 'ln_l_w': ln_l_w, 'ln_l_b': ln_l_b, 'Wq': Wq, 'Wkv': Wkv, 'Wout': Wout}
    _L0_xattn_all = _L0_xattn_setup()
    _L0_xattn_in = {k: v for k, v in _L0_xattn_all.items() if k in ('ln_m_w', 'ln_m_b', 'ln_l_w', 'ln_l_b', 'Wq', 'Wkv', 'Wout')}
    del _L0_xattn_all

    def _L0_ffn_setup():
        import jax, jax.numpy as jnp
        import numpy as np
        D_MODEL = 128
        key = jax.random.key(seed)
        k_x, k_w, k_a1, k_a2 = jax.random.split(key, 4)
        x = jax.random.normal(k_x, (4, 256, D_MODEL), dtype=jnp.float32)
        weight = jax.random.normal(k_w, (D_MODEL, D_MODEL), dtype=jnp.float32) * 0.02
        aux_weight1 = jax.random.normal(k_a1, (D_MODEL, D_MODEL), dtype=jnp.float32) * 0.02
        aux_weight2 = jax.random.normal(k_a2, (D_MODEL, D_MODEL), dtype=jnp.float32) * 0.02
        bias = jnp.zeros((D_MODEL,), dtype=jnp.float32)
        return {'x': x, 'weight': weight, 'aux_weight1': aux_weight1, 'aux_weight2': aux_weight2, 'bias': bias}
    _L0_ffn_all = _L0_ffn_setup()
    _L0_ffn_in = {k: v for k, v in _L0_ffn_all.items() if k in ('weight', 'aux_weight1', 'aux_weight2', 'bias')}
    del _L0_ffn_all

    def _L1_xattn_setup():
        import jax, jax.numpy as jnp
        import numpy as np
        B, NQ, NK = (4, 256, 256)
        QDIM = CDIM = 128
        H, DH = (16, 64)
        SCALE = DH ** (-0.5)
        WSTD = 0.02
        key = jax.random.key(seed)
        ks = jax.random.split(key, 6)
        inner = H * DH
        return {'x': jax.random.normal(ks[0], (B, NQ, QDIM), dtype=jnp.float32), 'context': jax.random.normal(ks[1], (B, NK, CDIM), dtype=jnp.float32), 'Wq': jax.random.normal(ks[2], (inner, QDIM), dtype=jnp.float32) * WSTD, 'Wk': jax.random.normal(ks[3], (inner, CDIM), dtype=jnp.float32) * WSTD, 'Wv': jax.random.normal(ks[4], (inner, CDIM), dtype=jnp.float32) * WSTD, 'Wo': jax.random.normal(ks[5], (QDIM, inner), dtype=jnp.float32) * WSTD, 'bo': jnp.zeros((QDIM,), dtype=jnp.float32)}
    _L1_xattn_all = _L1_xattn_setup()
    _L1_xattn_in = {k: v for k, v in _L1_xattn_all.items() if k in ('Wq', 'Wk', 'Wv', 'Wo', 'bo')}
    del _L1_xattn_all

    def _L1_ffn_setup():
        import jax, jax.numpy as jnp
        import numpy as np
        EPS = float(jnp.finfo(jnp.float32).eps)
        TOP_K = 2

        def rmsnorm(x, w):
            return x * jax.lax.rsqrt(jnp.mean(x * x, axis=-1, keepdims=True) + EPS) * w
        B, T, D_IN, D_MODEL, D_FF, D_OUT, E = (8, 128, 128, 128, 512, 128, 8)
        STD = 0.02
        key = jax.random.key(seed)
        ks = jax.random.split(key, 8)
        return {'s': jax.random.normal(ks[0], (B, T, D_IN), dtype=jnp.float32), 'W_in': STD * jax.random.normal(ks[1], (D_MODEL, D_IN), dtype=jnp.float32), 'in_norm_w': jnp.ones((D_MODEL,), dtype=jnp.float32), 'Wr': STD * jax.random.normal(ks[2], (E, D_MODEL), dtype=jnp.float32), 'expert_bias': jnp.zeros((E,), dtype=jnp.float32), 'Wg': STD * jax.random.normal(ks[3], (E, D_FF, D_MODEL), dtype=jnp.float32), 'Wu': STD * jax.random.normal(ks[4], (E, D_FF, D_MODEL), dtype=jnp.float32), 'Wd': STD * jax.random.normal(ks[5], (E, D_MODEL, D_FF), dtype=jnp.float32), 'enorm_w': jnp.ones((E, D_MODEL), dtype=jnp.float32), 'out_norm_w': jnp.ones((D_MODEL,), dtype=jnp.float32), 'W_out': STD * jax.random.normal(ks[6], (D_OUT, D_MODEL), dtype=jnp.float32)}
    _L1_ffn_all = _L1_ffn_setup()
    _L1_ffn_in = {k: v for k, v in _L1_ffn_all.items() if k in ('W_in', 'in_norm_w', 'Wr', 'expert_bias', 'Wg', 'Wu', 'Wd', 'enorm_w', 'out_norm_w', 'W_out')}
    del _L1_ffn_all
    return {'x': x, 'ctx_1024': ctx_1024, 'g_xattn': g_xattn, 'g_ffn': g_ffn, 'L0_xattn_ln_m_w': _L0_xattn_in['ln_m_w'], 'L0_xattn_ln_m_b': _L0_xattn_in['ln_m_b'], 'L0_xattn_ln_l_w': _L0_xattn_in['ln_l_w'], 'L0_xattn_ln_l_b': _L0_xattn_in['ln_l_b'], 'L0_xattn_Wq': _L0_xattn_in['Wq'], 'L0_xattn_Wkv': _L0_xattn_in['Wkv'], 'L0_xattn_Wout': _L0_xattn_in['Wout'], 'L0_ffn_weight': _L0_ffn_in['weight'], 'L0_ffn_aux_weight1': _L0_ffn_in['aux_weight1'], 'L0_ffn_aux_weight2': _L0_ffn_in['aux_weight2'], 'L0_ffn_bias': _L0_ffn_in['bias'], 'L1_xattn_Wq': _L1_xattn_in['Wq'], 'L1_xattn_Wk': _L1_xattn_in['Wk'], 'L1_xattn_Wv': _L1_xattn_in['Wv'], 'L1_xattn_Wo': _L1_xattn_in['Wo'], 'L1_xattn_bo': _L1_xattn_in['bo'], 'L1_ffn_W_in': _L1_ffn_in['W_in'], 'L1_ffn_in_norm_w': _L1_ffn_in['in_norm_w'], 'L1_ffn_Wr': _L1_ffn_in['Wr'], 'L1_ffn_expert_bias': _L1_ffn_in['expert_bias'], 'L1_ffn_Wg': _L1_ffn_in['Wg'], 'L1_ffn_Wu': _L1_ffn_in['Wu'], 'L1_ffn_Wd': _L1_ffn_in['Wd'], 'L1_ffn_enorm_w': _L1_ffn_in['enorm_w'], 'L1_ffn_out_norm_w': _L1_ffn_in['out_norm_w'], 'L1_ffn_W_out': _L1_ffn_in['W_out']}

def reference(x, ctx_1024, g_xattn, g_ffn, L0_xattn_ln_m_w, L0_xattn_ln_m_b, L0_xattn_ln_l_w, L0_xattn_ln_l_b, L0_xattn_Wq, L0_xattn_Wkv, L0_xattn_Wout, L0_ffn_weight, L0_ffn_aux_weight1, L0_ffn_aux_weight2, L0_ffn_bias, L1_xattn_Wq, L1_xattn_Wk, L1_xattn_Wv, L1_xattn_Wo, L1_xattn_bo, L1_ffn_W_in, L1_ffn_in_norm_w, L1_ffn_Wr, L1_ffn_expert_bias, L1_ffn_Wg, L1_ffn_Wu, L1_ffn_Wd, L1_ffn_enorm_w, L1_ffn_out_norm_w, L1_ffn_W_out):
    import jax
    import jax.numpy as jnp

    def _L0_xattn_ref(x, latents, ln_m_w, ln_m_b, ln_l_w, ln_l_b, Wq, Wkv, Wout):
        import jax, jax.numpy as jnp
        import numpy as np
        DIM = 128
        HEADS = 8
        DIM_HEAD = 64
        INNER = HEADS * DIM_HEAD
        EPS = 1e-05

        def layernorm(x, w, b):
            mu = jnp.mean(x, axis=-1, keepdims=True)
            var = jnp.var(x, axis=-1, keepdims=True)
            return (x - mu) * jax.lax.rsqrt(var + EPS) * w + b
        scale = DIM_HEAD ** (-0.5)
        xn = layernorm(x, ln_m_w, ln_m_b)
        ln = layernorm(latents, ln_l_w, ln_l_b)
        b = xn.shape[0]
        q = ln @ Wq
        kv_input = jnp.concatenate([xn, ln], axis=-2)
        kv = kv_input @ Wkv
        k, v = jnp.split(kv, 2, axis=-1)

        def to_heads(t):
            return t.reshape(b, t.shape[1], HEADS, DIM_HEAD).transpose(0, 2, 1, 3)
        q, k, v = (to_heads(q) * scale, to_heads(k), to_heads(v))
        sim = jnp.einsum('bhid,bhjd->bhij', q, k)
        attn = jax.nn.softmax(sim, axis=-1)
        out = jnp.einsum('bhij,bhjd->bhid', attn, v)
        out = out.transpose(0, 2, 1, 3).reshape(b, out.shape[2], INNER)
        return out @ Wout

    def _L0_ffn_ref(x, weight, aux_weight1, aux_weight2, bias):
        import jax, jax.numpy as jnp
        import numpy as np
        D_MODEL = 128
        h = jnp.einsum('btc,cd->btd', x, weight)
        h = jnp.einsum('btc,cd->btd', h, aux_weight1)
        h = jnp.einsum('btc,cd->btd', h, aux_weight2)
        return jnp.tanh(h + bias)

    def _L1_xattn_ref(x, context, Wq, Wk, Wv, Wo, bo):
        import jax, jax.numpy as jnp
        import numpy as np
        B, NQ, NK = (4, 256, 256)
        QDIM = CDIM = 128
        H, DH = (16, 64)
        SCALE = DH ** (-0.5)
        WSTD = 0.02
        b, nq, _ = x.shape
        nk = context.shape[1]
        q = (x @ Wq.T).reshape(b, nq, H, DH)
        k = (context @ Wk.T).reshape(b, nk, H, DH)
        v = (context @ Wv.T).reshape(b, nk, H, DH)
        sim = jnp.einsum('bihd,bjhd->bhij', q, k) * SCALE
        attn = jax.nn.softmax(sim, axis=-1)
        out = jnp.einsum('bhij,bjhd->bihd', attn, v).reshape(b, nq, H * DH)
        return out @ Wo.T + bo

    def _L1_ffn_ref(s, W_in, in_norm_w, Wr, expert_bias, Wg, Wu, Wd, enorm_w, out_norm_w, W_out):
        import jax, jax.numpy as jnp
        import numpy as np
        EPS = float(jnp.finfo(jnp.float32).eps)
        TOP_K = 2

        def rmsnorm(x, w):
            return x * jax.lax.rsqrt(jnp.mean(x * x, axis=-1, keepdims=True) + EPS) * w
        B, T, _ = s.shape
        x = s.reshape(B * T, -1)
        h = rmsnorm(x @ W_in.T, in_norm_w)
        logits = h @ Wr.T
        _, idx = jax.lax.top_k(logits + expert_bias, TOP_K)
        sel = jnp.take_along_axis(logits, idx, axis=-1)
        g_topk = jax.nn.softmax(sel, axis=-1)
        N = logits.shape[0]
        gates = jnp.zeros_like(logits).at[jnp.arange(N)[:, None], idx].set(g_topk)
        out = jnp.zeros_like(h)
        for e in range(Wg.shape[0]):
            gate = jax.nn.silu(h @ Wg[e].T)
            up = h @ Wu[e].T
            oe = rmsnorm(gate * up @ Wd[e].T, enorm_w[e])
            out = out + gates[:, e:e + 1] * oe
        s_hat = rmsnorm(out, out_norm_w) @ W_out.T
        return s_hat.reshape(B, T, -1)
    x = x + jnp.tanh(g_xattn[0]) * _L0_xattn_ref(ctx_1024, _layernorm(x, axis=-1), L0_xattn_ln_m_w, L0_xattn_ln_m_b, L0_xattn_ln_l_w, L0_xattn_ln_l_b, L0_xattn_Wq, L0_xattn_Wkv, L0_xattn_Wout)
    x = x + jnp.tanh(g_ffn[0]) * _L0_ffn_ref(_layernorm(x, axis=-1), L0_ffn_weight, L0_ffn_aux_weight1, L0_ffn_aux_weight2, L0_ffn_bias)
    x = x + jnp.tanh(g_xattn[1]) * _L1_xattn_ref(_layernorm(x, axis=-1), ctx_1024, L1_xattn_Wq, L1_xattn_Wk, L1_xattn_Wv, L1_xattn_Wo, L1_xattn_bo)
    x = x + jnp.tanh(g_ffn[1]) * _L1_ffn_ref(_layernorm(x, axis=-1), L1_ffn_W_in, L1_ffn_in_norm_w, L1_ffn_Wr, L1_ffn_expert_bias, L1_ffn_Wg, L1_ffn_Wu, L1_ffn_Wd, L1_ffn_enorm_w, L1_ffn_out_norm_w, L1_ffn_W_out)
    return x

_drawn_inputs = setup_inputs


def setup_inputs(seed=0):
    import zlib

    import numpy as np

    out = dict(_drawn_inputs(seed))
    spreads = {'g_ffn': (-1.0, 0.6),
     'L0_xattn_ln_m_w': (1.0, 0.2),
     'L0_xattn_ln_m_b': (0.0, 0.1),
     'L0_xattn_ln_l_w': (1.0, 0.2),
     'L0_xattn_ln_l_b': (0.0, 0.28),
     'L0_ffn_bias': (0.0, 0.1),
     'L1_xattn_bo': (0.0, 0.1),
     'L1_ffn_in_norm_w': (1.0, 0.2),
     'L1_ffn_expert_bias': (0.0, 0.1),
     'L1_ffn_enorm_w': (1.0, 0.2),
     'L1_ffn_out_norm_w': (1.0, 0.2)}
    factors = {'L0_ffn_weight': 3.673,
     'L0_ffn_aux_weight1': 3.247,
     'L0_ffn_aux_weight2': 3.595,
     'L1_xattn_Wq': 8.0,
     'L1_xattn_Wk': 7.9}
    for name, (base, spread) in spreads.items():
        noise = np.random.default_rng([zlib.crc32(name.encode()), seed]).standard_normal(out[name].shape)
        drawn = base * np.exp(spread * noise) if base else spread * noise
        out[name] = jnp.asarray(drawn.astype(out[name].dtype))
    for name, factor in factors.items():
        out[name] = (out[name] * factor).astype(out[name].dtype)
    return out
```

```python
from contextlib import ExitStack

import concourse.bass as bass
from concourse import mybir

F32 = mybir.dt.float32
F16 = mybir.dt.float16
ALU = mybir.AluOpType
ACT = mybir.ActivationFunctionType
AX = mybir.AxisListType

P = 128
B, NQ, C = 16, 100, 128
NK = 1444
KT = (NK + P - 1) // P
KLAST = NK - (KT - 1) * P
CH = NK // 4
DH = 64
LN_EPS = 1e-5
RMS_EPS = 1.1920928955078125e-07
E, FF = 8, 512
FT = FF // P
WSCALE = 256.0
GROUP = 4


class Layer:

    def __init__(self, index, heads, with_latents):
        self.index = index
        self.heads = heads
        self.lat = with_latents
        self.T = (heads * NQ + P - 1) // P
        self.N = 2 * self.T
        self.KT = KT + (1 if with_latents else 0)
        self.groups = (self.KT + GROUP - 1) // GROUP
        self.qgroups = heads // GROUP
        self.maxes = 3 if with_latents else 2
        self.values_at = 3 if with_latents else 2
        self.sums = 3 if with_latents else 2
        first_q, first_x = (1, 3) if with_latents else (2, 7)
        self.sched = [[] for _ in range(self.N + 2)]
        for n in range(self.N + 2):
            if n >= 2:
                self.sched[n].append(("Z", None, n - 2))
            if n == self.T + 2:
                self.sched[n].append(("O", 0, 0))
            if n == self.N + 1:
                self.sched[n].append(("O", 1, 0))
            if n < self.N:
                t, into = n % self.T, 1 - n // self.T
                if first_q <= t < first_q + self.qgroups:
                    self.sched[n].append(("Q", into, t - first_q))
                if first_x <= t < first_x + 3:
                    self.sched[n].append(("X", into, t - first_x))
        self.prologue = [("Q", 0, k) for k in range(self.qgroups)] + [("X", 0, k) for k in range(3)]
        flat = [s for step in self.sched for s in step]
        self.pieces = len(flat)
        self.flat = flat


L0 = Layer(0, 8, True)
L1 = Layer(1, 16, False)
LOOPS = B // 2


class Count:

    def __init__(self, per0, per1, units0, credit=0):
        self.per, self.base = (per0, per1), (credit, credit + per0 * units0)

    def at(self, layer, i, unit, per_loop, k):
        per = self.per[layer.index]
        return i * (per * per_loop) + (self.base[layer.index] + per * unit + k)


def flamingo_kernel(nc, a):
    ctx = ExitStack()
    with ctx:
        def sb(name, shape, dt=F32):
            return ctx.enter_context(nc.sbuf_tensor(name, shape, dt))

        def sem(name):
            return ctx.enter_context(nc.semaphore(name))

        x = sb("x", [P, B, C])
        xq = sb("xq", [P, B + 1, C])
        xqT = sb("xqT", [P, (B + 1) * NQ])
        tmp = sb("tmp", [P, B, C])
        raw = sb("raw", [P, 2, KT, C])
        Xhi = sb("Xhi", [P, 2, KT + 1, C], F16)
        Xlo = sb("Xlo", [P, 2, KT + 1, C], F16)
        KW = (KT + 1) * P
        XThi = sb("XThi", [P, 2, KW], F16)
        XTlo = sb("XTlo", [P, 2, KW], F16)
        QW = L1.T * P
        QThi = sb("QThi", [P, 2, QW], F16)
        QTlo = sb("QTlo", [P, 2, QW], F16)
        prob = sb("prob", [P, 2, KW])
        PThi = sb("PThi", [P, 2, KW], F16)
        PTlo = sb("PTlo", [P, 2, KW], F16)
        Zs = sb("Zs", [P, 2, C])
        ZT = sb("ZT", [P, 2, QW])
        Amat = sb("Amat", [P, L0.heads + L1.heads, C])
        Mmat = sb("Mmat", [P, L0.heads + L1.heads, C])
        ident = sb("ident", [P, P])
        mx = sb("mx", [P, 2, 4])
        negm = sb("negm", [P, 2])
        lsum = sb("lsum", [P, 2, 4])
        lall = sb("lall", [P, 2])
        rinv = sb("rinv", [P, 2])
        stat6 = sb("stat6", [P, KT, 6])
        mv = sb("mv", [P, KT, 2])
        rstd_k = sb("rstd_k", [P, KT])
        nmean_k = sb("nmean_k", [P, KT])
        lnmw = sb("lnmw", [P, C])
        lnmb = sb("lnmb", [P, C])
        lnlw = sb("lnlw", [P, C])
        lnlb = sb("lnlb", [P, C])
        fbias = sb("fbias", [P, C])
        obias = sb("obias", [P, C])
        innw = sb("innw", [P, C])
        outnw = sb("outnw", [P, C])
        enw = sb("enw", [P, E, C])
        ebias = sb("ebias", [P, E])
        gin = sb("gin", [P, 4])
        gt = sb("gt", [P, 4])
        small = sb("small", [P, 8, B])
        Wsm = sb("Wsm", [P, 6, C])
        WsmT = sb("WsmT", [P, 4, C])
        Wf = sb("Wf", [P, 2, C])
        route = sb("route", [P, 8, B * E])
        iota8 = sb("iota8", [P, E])
        var_k = sb("var_k", [P, KT])
        minus_half = sb("minus_half", [P, B])
        coef = sb("coef", [P, 2, 3, GROUP])
        ssq = sb("ssq", [P, 2, GROUP])
        hThi, hTlo = QThi[:, 0, :], QTlo[:, 0, :]
        wThi, wTlo = (w[:, :, 0:3 * FT * P].rearrange("p b (k f) -> p b k f", k=3) for w in (XThi, XTlo))
        ahi, alo = (w[:, :, 0:FT * 4 * NQ].rearrange("p b (f n) -> p b f n", f=FT) for w in (PThi, PTlo))
        sil, actf = prob[:, :, 0:4 * NQ], prob[:, :, 4 * NQ:8 * NQ]
        sqs, term = (ZT[:, :, s * 512:(s + 1) * 512].rearrange("p b (s c) -> p b s c", c=C) for s in range(2))
        LATC = slice(KT * P, KT * P + NQ)

        wraw = sb("wraw", [P, 48, C])
        wT = sb("wT", [P, 20, C])

        score = ctx.enter_context(nc.psum_tensor("score", [P, 4, 512], F32))
        turn = ctx.enter_context(nc.psum_tensor("turn", [P, 2, 512], F32))
        vbank = ctx.enter_context(nc.psum_tensor("vbank", [P, 512], F32))
        side = ctx.enter_context(nc.psum_tensor("side", [P, 512], F32))

        S = {n: sem(n) for n in """waited var_ready rstd_ready ms_ready coef_ready acc_ready act_ready ahi_ready alo_ready coef_step ctx_in0 ctx_in1 down_ready dve_chain
            exp_done ffn_biased ffn_tanh fold_done fold_ready gates_tanh glue_T_done
            glue_T_ready gu_ready h_hi h_split ident_ready logits_ready max_part moe_in0
            moe_in1 negm_ready normed out_in params_in piece_done piece_hi piece_ready
            pt_hi pt_lo rinv_ready route_exp route_ready scaled score_ready sil_ready
            small_done small_ready sq_ready stat_step stats_ready sum_ready token_mm
            turned v_ready values_done values_hi w_hi w_lo w_turned weights_in x_final
            x_in xq_ready z_scaled zeros_ready""".split()}

        score_c = Count(2, 2, B * L0.T)
        exp_c = Count(2, 2, B * L0.T, credit=2)
        turned_c = Count(L0.groups, L1.groups, B * L0.T)
        pthi_c = Count(L0.groups, L1.groups, B * L0.T)
        ptlo_c = Count(L0.groups, L1.groups, B * L0.T, credit=2)
        v_c = Count(1, 1, B * L0.T, credit=2)
        z_c = Count(1, 1, B * L0.T, credit=1)
        tile_c = Count(1, 1, B * L0.T)

        class PieceCount:

            def __init__(self, kinds):
                def n(seq):
                    return sum(s[0] in kinds for s in seq)
                self.kinds = kinds
                self.loop = (n(L0.flat), n(L1.flat))
                self.pro = (n(L0.prologue), n(L1.prologue))
                self.start = (0, self.pro[0] + LOOPS * self.loop[0])

            def prologue(self, layer, m):
                return self.start[layer.index] + sum(s[0] in self.kinds for s in layer.prologue[:m])

            def at(self, layer, i, m):
                done = sum(s[0] in self.kinds for s in layer.flat[:m])
                return i * self.loop[layer.index] + (self.start[layer.index] + self.pro[layer.index] + done)

        every = PieceCount("ZOQX")
        split = PieceCount("QX")

        def operands_complete(layer, par):
            last = [m for m, s in enumerate(layer.flat) if s[0] in "QX" and s[1] == par]
            return max(last) + 1

        PREPARED = B + 1

        def prepared(layer, i, ahead, per=1):
            return i * (2 * per) + (PREPARED * layer.index + ahead + 1) * per

        def loaded(layer, i, ahead):
            if ahead % 2:
                return i * 32 + (LOOPS * layer.index + 1) * 32
            return i * 32 + ((LOOPS + 1) * layer.index + ahead // 2 + 1) * 32

        GLUE = B // GROUP
        CHUNKS, UNITS = 8, 8 * FT
        PARAMS, WEIGHTS = 12, 13

        def half(block, h):
            return block[(h % 2) * DH:(h % 2 + 1) * DH, :]

        def fold_groups():
            def turns(src, dst):
                return (0, wT[:, dst:dst + 4, :], 1.0, [(wraw[:, src + s, :], None) for s in range(4)])
            out = [turns(0, 0), turns(4, 4), turns(8, 8), turns(40, 12), turns(44, 16)]
            for L, lq, lk, lv, lo in ((L0, (wT, 0), (wT, 4), (wT, 8), (wraw, 12)),
                                      (L1, (wraw, 16), (wraw, 24), (wraw, 32), (wT, 12))):
                first = L0.heads * L.index
                for dst, l, r, need, scale in ((Amat, lq, lk, 2, DH ** -0.5),
                                               (Mmat, lv, lo, 5, gt[:, L.index:L.index + 1])):
                    for h0 in [g * 8 + par for g in range(L.heads // 8) for par in range(2)]:
                        out.append((need, dst[:, first + h0:first + h0 + 7:2, :], scale,
                                    [(half(l[0][:, l[1] + h // 2, :], h), half(r[0][:, r[1] + h // 2, :], h))
                                     for h in range(h0, h0 + 8, 2)]))
            return out

        FOLD = fold_groups()
        FOLDS = len(FOLD)

        def qcols(k):
            return slice(k * GROUP * NQ, (k + 1) * GROUP * NQ)

        block = ctx.enter_context(nc.Block())

        @block.sync
        def _(sp):
            def row(v):
                return v.rearrange("(a c) -> a c", a=1)

            sp.dma_start(x[:NQ, :, :], a["x"].rearrange("b q c -> q b c")).then_inc(S["x_in"], 16)
            for dst, src in ((lnlw, "L0_xattn_ln_l_w"), (lnlb, "L0_xattn_ln_l_b"), (lnmw, "L0_xattn_ln_m_w"),
                             (lnmb, "L0_xattn_ln_m_b"), (fbias, "L0_ffn_bias"), (obias, "L1_xattn_bo"),
                             (innw, "L1_ffn_in_norm_w"), (outnw, "L1_ffn_out_norm_w"),
                             (ebias, "L1_ffn_expert_bias")):
                sp.dma_start(dst[:, :], row(a[src]).to_broadcast([P, dst.shape[1]])).then_inc(S["params_in"], 16)
            sp.dma_start(gin[:, 0:2], row(a["g_xattn"]).to_broadcast([P, 2])).then_inc(S["params_in"], 16)
            sp.dma_start(gin[:, 2:4], row(a["g_ffn"]).to_broadcast([P, 2])).then_inc(S["params_in"], 16)
            sp.dma_start(enw[:, :, :], a["L1_ffn_enorm_w"].rearrange("(a e) d -> a e d", a=1)
                         .to_broadcast([P, E, C])).then_inc(S["params_in"], 16)
            for at, n, src in ((0, 4, a["L0_xattn_Wq"].rearrange("c (k e) -> c k e", e=P)),
                               (4, 8, a["L0_xattn_Wkv"].rearrange("c (k e) -> c k e", e=P)),
                               (12, 4, a["L0_xattn_Wout"].rearrange("(k e) c -> e k c", e=P)),
                               (16, 8, a["L1_xattn_Wq"].rearrange("(k e) c -> e k c", e=P)),
                               (24, 8, a["L1_xattn_Wk"].rearrange("(k e) c -> e k c", e=P)),
                               (32, 8, a["L1_xattn_Wv"].rearrange("(k e) c -> e k c", e=P)),
                               (40, 8, a["L1_xattn_Wo"].rearrange("c (k e) -> c k e", e=P))):
                sp.dma_start(wraw[:, at:at + n, :], src).then_inc(S["weights_in"], 16)
            for s, w in enumerate(("L0_ffn_weight", "L0_ffn_aux_weight1", "L0_ffn_aux_weight2",
                                   "L1_ffn_W_in", "L1_ffn_W_out")):
                sp.dma_start(Wsm[:, s, :], a[w]).then_inc(S["weights_in"], 16)
            sp.dma_start(Wsm[0:E, 5, :], a["L1_ffn_Wr"]).then_inc(S["weights_in"], 16)

            def load(src, par):
                full = src[0:(KT - 1) * P, :].rearrange("(t p) c -> p t c", p=P)
                sp.dma_start(raw[:, par, 0:KT - 1, :], full).then_inc(S[f"ctx_in{par}"], 16)
                sp.dma_start(raw[:KLAST, par, KT - 1, :], src[(KT - 1) * P:NK, :]).then_inc(S[f"ctx_in{par}"], 16)

            c = a["ctx_1024"]
            sp.wait_ge(S["zeros_ready"], 1)
            for L in (L0, L1):
                if L is L1:
                    sp.wait_ge(S["values_done"], prepared(L0, LOOPS - 1, 2))
                    sp.wait_ge(S["piece_done"], every.at(L0, LOOPS - 1, L0.pieces))
                load(c[0], 0)
                load(c[1], 1)
                with sp.Fori(0, LOOPS - 1) as i:
                    for par in range(2):
                        sp.wait_ge(S["values_done"], prepared(L, i, par))
                        sp.sem_inc(S["waited"], 1)
                        m = operands_complete(L, 1) if par else 0
                        sp.wait_ge(S["piece_done"], every.at(L, i, m))
                        sp.sem_inc(S["waited"], 1)
                        load(c[bass.ds(2 * i + 2 + par, 1), :, :].rearrange("a k c -> (a k) c"), par)
                sp.wait_ge(S["values_done"], prepared(L, LOOPS - 1, 0))
                sp.wait_ge(S["piece_done"], every.at(L, LOOPS - 1, 0))
                load(c[0], 0)

            def load_expert(ep, e):
                for at, src in ((0, a["L1_ffn_Wg"][bass.ds(e, 1)].rearrange("a (k p) d -> p (a k) d", p=P)),
                                (4, a["L1_ffn_Wu"][bass.ds(e, 1)].rearrange("a (k p) d -> p (a k) d", p=P)),
                                (8, a["L1_ffn_Wd"][bass.ds(e, 1)].rearrange("a o (k p) -> o (a k) p", p=P))):
                    at += ep * 3 * FT
                    sp.dma_start(wraw[:, at:at + FT, :], src).then_inc(S[f"moe_in{ep}"], 16)

            sp.wait_ge(S["fold_done"], FOLDS)
            load_expert(0, 0)
            load_expert(1, 1)
            with sp.Fori(0, E // 2 - 1) as i:
                for ep in range(2):
                    sp.wait_ge(S["w_lo"], i * 6 + 3 * (ep + 1))
                    sp.sem_inc(S["waited"], 1)
                    load_expert(ep, 2 * i + 2 + ep)
            sp.wait_ge(S["w_lo"], 3 * (E - 1))
            load_expert(0, 0)
            sp.wait_ge(S["moe_in0"], 48 * (E // 2 + 1))
            sp.wait_ge(S["x_final"], 1)
            sp.dma_start(a["out"].rearrange("b q c -> q b c"), x[:NQ, :, :]).then_inc(S["out_in"], 16)
            sp.wait_ge(S["out_in"], 16)

        @block.gpsimd
        def _(pool):
            pool.sem_inc(S["alo_ready"], 1)
            nc.gpsimd.memset(ident[:, :], 0.0).then_inc(S["ident_ready"], 1)
            pool.wait_ge(S["ident_ready"], 1)
            nc.gpsimd.affine_select(out=ident[:, :], in_=ident[:, :], compare_op=ALU.not_equal, fill=1.0, base=0,
                                    pattern=[[-1, P]], channel_multiplier=1).then_inc(S["ident_ready"], 1)
            for par in range(2):
                nc.gpsimd.memset(raw[:, par, KT - 1, :], 0.0)
                nc.gpsimd.memset(Xhi[:, par, KT, :], 0.0)
                nc.gpsimd.memset(Xlo[:, par, KT, :], 0.0)
                nc.gpsimd.memset(prob[:, par, NK:KW], 0.0)
                nc.gpsimd.memset(QThi[:, par, :], 0.0)
                nc.gpsimd.memset(QTlo[:, par, :], 0.0)
            nc.gpsimd.memset(minus_half[:, :], -0.5)
            nc.gpsimd.memset(xq[:, B, :], 0.0)
            nc.gpsimd.memset(xqT[:, B * NQ:], 0.0)
            for e in range(E):
                last = nc.gpsimd.memset(iota8[:, e:e + 1], float(e - E))
            last.then_inc(S["zeros_ready"], 1)

            def prepare(L, i, ahead, bq):
                par = ahead % 2
                X = raw[:, par, :, :]
                done = prepared(L, i, ahead)
                if L.lat:
                    pool.wait_ge(S["stats_ready"], done)
                    nc.gpsimd.tensor_tensor(rstd_k[:, :], var_k[:, :], minus_half[:, 0:KT], ALU.pow).then_inc(S["scaled"], 1)
                    pool.wait_ge(S["scaled"], prepared(L, i, ahead, 3) - 2)
                    pool.sem_inc(S["waited"], 1)
                    for t in range(KT):
                        last = nc.gpsimd.tensor_scalar(raw[:, par, t, :], raw[:, par, t, :], nmean_k[:, t:t + 1],
                                                       rstd_k[:, t:t + 1], ALU.add, ALU.mult)
                    last.then_inc(S["scaled"], 1)
                    pool.wait_ge(S["scaled"], prepared(L, i, ahead, 3) - 1)
                    nc.gpsimd.tensor_tensor(X, X, lnmw[:, :].unsqueeze(1).to_broadcast([P, KT, C]),
                                            ALU.mult).then_inc(S["scaled"], 1)
                    pool.wait_ge(S["scaled"], prepared(L, i, ahead, 3))
                    nc.gpsimd.tensor_tensor(X, X, lnmb[:, :].unsqueeze(1).to_broadcast([P, KT, C]),
                                            ALU.add).then_inc(S["normed"], 1)
                    pool.wait_ge(S["normed"], done)
                pool.wait_ge(S["values_hi"], done)
                last = nc.gpsimd.tensor_tensor(Xlo[:, par, 0:KT, :], X, Xhi[:, par, 0:KT, :], ALU.subtract)
                if L.lat:
                    nc.gpsimd.tensor_tensor(Xlo[:NQ, par, KT, :],
                                            xq[:NQ, bass.ds(bq, 1), :].rearrange("p a c -> p (a c)"),
                                            Xhi[:NQ, par, KT, :], ALU.subtract)
                    last = nc.gpsimd.tensor_tensor(XTlo[:, par, LATC], xqT[:, bass.ds(bq * NQ, NQ)],
                                                   XThi[:, par, LATC], ALU.subtract)
                last.then_inc(S["values_done"], 1)

            def power(n):
                pool.wait_ge(S["var_ready"], n)
                nc.gpsimd.tensor_tensor(small[:NQ, 2, :], small[:NQ, 1, :], minus_half[:NQ, :],
                                        ALU.pow).then_inc(S["rstd_ready"], 1)

            pool.wait_ge(S["zeros_ready"], 1)
            power(1)
            power(2)
            pool.wait_ge(S["params_in"], 16 * PARAMS)
            for L in (L0, L1):
                if L is L1:
                    power(3)
                    power(4)
                if L.lat:
                    pool.wait_ge(S["glue_T_done"], GLUE)
                prepare(L, 0, 0, 0)
                with pool.Fori(0, LOOPS) as i:
                    prepare(L, i, 1, 2 * i + 1)
                    prepare(L, i, 2, 2 * i + 2)

            power(5)
            power(6)
            with pool.Fori(0, E // 2) as i:
                for J in range(CHUNKS + 1):
                    for f in range(FT):
                        if J < CHUNKS:
                            u = J * FT + f
                            pool.wait_ge(S["ahi_ready"], i * UNITS + u + 1)
                            nc.gpsimd.tensor_tensor(alo[:, J % 2, f, :], actf[:, u % 2, :], ahi[:, J % 2, f, :],
                                                    ALU.subtract).then_inc(S["alo_ready"], 1)
                    if J >= 1:
                        d = (J - 1) % 2
                        pool.wait_ge(S["ms_ready"], i * CHUNKS + J)
                        nc.gpsimd.tensor_tensor(coef[:NQ, d, 1, :], coef[:NQ, d, 0, :], minus_half[:NQ, 0:GROUP],
                                                ALU.pow).then_inc(S["coef_ready"], 1)
            power(7)

        @block.tensor
        def _(pe):
            mm, tr = nc.tensor.matmul, nc.tensor.transpose
            pe.sem_inc(S["v_ready"], 2)
            pe.sem_inc(S["down_ready"], 2)

            pe.wait_ge(S["ident_ready"], 2)
            pe.wait_ge(S["weights_in"], 16 * WEIGHTS)
            for n, group in enumerate(FOLD):
                if n >= 4:
                    pe.wait_ge(S["fold_done"], n - 3)
                needs, _, _, members = group
                pe.wait_ge(S["fold_done"], needs)
                for s, (l, r) in enumerate(members):
                    o = score[:, n % 4, s * P:(s + 1) * P]
                    last = tr(o, l, ident[:, :]) if r is None else mm(o, l, r, start=True, stop=True)
                last.then_inc(S["fold_ready"], 1)
            for s, m in enumerate((0, 3, 4)):
                tr(side[:, s * P:(s + 1) * P], Wsm[:, m, :], ident[:, :])
            tr(side[:, 3 * P:3 * P + E], Wsm[0:E, 5, :], ident[0:E, 0:E]).then_inc(S["small_ready"], 1)
            pe.wait_ge(S["small_done"], 1)
            mm(side[:, 0:P], Wsm[:, 1, :], WsmT[:, 0, :], start=True, stop=True).then_inc(S["small_ready"], 1)
            pe.wait_ge(S["small_done"], 2)
            mm(side[:, 0:P], Wf[:, 0, :], Wsm[:, 2, :], start=True, stop=True).then_inc(S["small_ready"], 1)
            pe.wait_ge(S["small_done"], 3)

            def glue_transposes(n):
                for k in range(GLUE):
                    pe.wait_ge(S["xq_ready"], n + 1)
                    for s in range(GROUP):
                        b = k * GROUP + s
                        last = tr(score[:, k, s * NQ:(s + 1) * NQ], xq[:NQ, b, :], ident[:NQ, :NQ])
                    last.then_inc(S["glue_T_ready"], 1)

            pe.wait_ge(S["fold_done"], FOLDS)
            glue_transposes(0)
            pe.wait_ge(S["glue_T_done"], GLUE)

            def attention(L):
                A0 = 0 if L.lat else L0.heads

                def piece(i, idx, kind, par, k, bq):
                    pe.wait_ge(S["piece_done"], idx)
                    if kind == "Q":
                        for s in range(GROUP):
                            last = mm(side[:, s * NQ:(s + 1) * NQ], Amat[:, A0 + k * GROUP + s, :],
                                      xqT[:, bass.ds(bq * NQ, NQ)] if i is not None else xqT[:, 0:NQ],
                                      start=True, stop=True)
                    elif kind == "X":
                        for s in range(GROUP):
                            last = tr(side[:, s * P:(s + 1) * P], raw[:, par, k * GROUP + s, :], ident[:, :])
                    elif kind == "Z":
                        last = tr(side[:, 0:P], Zs[:, k % 2, :], ident[:, :])
                    else:
                        for h in range(L.heads):
                            last = mm(side[:NQ, 0:C], ZT[:, par, h * NQ:(h + 1) * NQ], Mmat[:, A0 + h, :],
                                      start=(h == 0), stop=(h == L.heads - 1))
                    last.then_inc(S["piece_ready"], 1)

                for m, (kind, par, k) in enumerate(L.prologue):
                    if kind == "X":
                        if L.lat:
                            pe.wait_ge(S["normed"], prepared(L, 0, 0))
                        else:
                            pe.wait_ge(S["ctx_in0"], loaded(L, 0, 0))
                    piece(None, every.prologue(L, m), kind, par, k, 0)

                with pe.Fori(0, LOOPS) as i:
                    m = 0
                    for n in range(L.N + 2):
                        bp, t, p = n // L.T, n % L.T, n % 2

                        def turn_group(k):
                            q = (n - 1) % 2
                            G = (n - 1) * L.groups + k
                            pe.wait_ge(S["exp_done"], exp_c.at(L, i, n - 1, L.N, 2 if k else 1))
                            pe.wait_ge(S["pt_lo"], ptlo_c.at(L, i, n - 1, L.N, k - 1))
                            for s in range(min(GROUP, L.KT - k * GROUP)):
                                kt = k * GROUP + s
                                last = tr(turn[:, G % 2, s * P:(s + 1) * P], prob[:, q, kt * P:(kt + 1) * P],
                                          ident[:, :])
                            last.then_inc(S["turned"], 1)

                        if n < L.N:
                            if t == 0:
                                if bp == 0:
                                    pe.wait_ge(S["piece_done"], every.at(L, i, 0))
                                else:
                                    pe.wait_ge(S["piece_done"], every.at(L, i, operands_complete(L, 1)))
                                pe.wait_ge(S["values_done"], prepared(L, i, bp))
                            qh, ql = (w[:, bp, t * P:(t + 1) * P] for w in (QThi, QTlo))
                            for c in range(4):
                                if c % 2 == 0:
                                    pe.wait_ge(S["exp_done"], exp_c.at(L, i, n - 1, L.N, c // 2 + 1))
                                parts = [(slice(0, CH), slice(c * CH, (c + 1) * CH))]
                                if L.lat and c == 3:
                                    parts.append((slice(CH, CH + NQ), LATC))
                                for o, s in parts:
                                    out = score[:, c, o]
                                    mm(out, qh, XThi[:, bp, s], start=True, stop=False)
                                    mm(out, qh, XTlo[:, bp, s], start=False, stop=False)
                                    last = mm(out, ql, XThi[:, bp, s], start=False, stop=True)
                                if c % 2:
                                    last.then_inc(S["score_ready"], 1)
                                if n >= 1 and c < L.groups:
                                    turn_group(c)
                        elif n == L.N:
                            for k in range(L.groups):
                                turn_group(k)
                        if 1 <= n <= L.N:
                            q, vp = (n - 1) % 2, (n - 1) // L.T
                            pe.wait_ge(S["z_scaled"], z_c.at(L, i, n - 1, L.N, 0))
                            for kt in range(L.KT):
                                if kt % GROUP == 0:
                                    pe.wait_ge(S["pt_lo"], ptlo_c.at(L, i, n - 1, L.N, kt // GROUP + 1))
                                ph, pl = (w[:, q, kt * P:(kt + 1) * P] for w in (PThi, PTlo))
                                mm(vbank[:, 0:C], ph, Xhi[:, vp, kt, :], start=(kt == 0), stop=False)
                                mm(vbank[:, 0:C], ph, Xlo[:, vp, kt, :], start=False, stop=False)
                                last = mm(vbank[:, 0:C], pl, Xhi[:, vp, kt, :], start=False, stop=(kt == L.KT - 1))
                            last.then_inc(S["v_ready"], 1)
                        for kind, par, k in L.sched[n]:
                            if kind == "Z":
                                pe.wait_ge(S["z_scaled"], z_c.at(L, i, k, L.N, 1))
                            if kind == "X":
                                ahead = 2 - par
                                if L.lat:
                                    pe.wait_ge(S["normed"], prepared(L, i, ahead))
                                else:
                                    pe.wait_ge(S[f"ctx_in{par}"], loaded(L, i, ahead))
                            piece(i, every.at(L, i, m), kind, par, k, 2 * i + (2 - par) if kind == "Q" else None)
                            m += 1

            attention(L0)

            glue_transposes(1)
            pe.wait_ge(S["glue_T_done"], 2 * GLUE)

            def token_matmul(weights):
                for k in range(GLUE):
                    for s in range(GROUP):
                        b = k * GROUP + s
                        last = mm(score[:NQ, k, s * P:(s + 1) * P], xqT[:, b * NQ:(b + 1) * NQ], weights,
                                  start=True, stop=True)
                    last.then_inc(S["token_mm"], 1)

            token_matmul(Wf[:, 1, :])
            glue_transposes(2)
            pe.wait_ge(S["glue_T_done"], 3 * GLUE)
            attention(L1)

            glue_transposes(3)
            pe.wait_ge(S["glue_T_done"], 4 * GLUE)
            token_matmul(WsmT[:, 1, :])
            glue_transposes(4)
            pe.wait_ge(S["glue_T_done"], 5 * GLUE)
            for b in range(B):
                last = mm(vbank[:NQ, b * E:(b + 1) * E], xqT[:, b * NQ:(b + 1) * NQ], WsmT[:, 3, 0:E],
                          start=True, stop=True)
            last.then_inc(S["logits_ready"], 1)

            def turn_weights(ep, k, value, arrived):
                pe.wait_ge(S[f"moe_in{ep}"], arrived)
                pe.wait_ge(S["w_lo"], value)
                for s in range(FT):
                    last = tr(side[:, s * P:(s + 1) * P], wraw[:, (ep * 3 + k) * FT + s, :], ident[:, :])
                last.then_inc(S["w_turned"], 1)

            for k in range(3):
                turn_weights(0, k, k, 48)
            pe.wait_ge(S["h_split"], 1)
            with pe.Fori(0, E // 2) as i:
                for J in range(CHUNKS + 1):
                    for f in range(FT):
                        if J < CHUNKS:
                            ep, j, u = J // 4, J % 4, J * FT + f
                            if u % (4 * FT) == 0:
                                pe.wait_ge(S["w_lo"], i * 6 + 3 * ep + 3)
                            pe.wait_ge(S["act_ready"], i * UNITS + u + 1)
                            cols = slice(j * 4 * NQ, (j + 1) * 4 * NQ)
                            for w in range(2):
                                out = score[:, (u % 2) * 2 + w, 0:4 * NQ]
                                wh, wl = (v[:, ep, w, f * P:(f + 1) * P] for v in (wThi, wTlo))
                                mm(out, wh, hThi[:, cols], start=True, stop=False)
                                mm(out, wh, hTlo[:, cols], start=False, stop=False)
                                last = mm(out, wl, hThi[:, cols], start=False, stop=True)
                            last.then_inc(S["gu_ready"], 1)
                        if J >= 1:
                            D, s = J - 1, f
                            ep = D // 4
                            if s == 0:
                                pe.wait_ge(S["alo_ready"], i * UNITS + D * FT + FT + 1)
                                pe.wait_ge(S["acc_ready"], i * CHUNKS + D + 1)
                            toks = slice(s * NQ, (s + 1) * NQ)
                            out = turn[:NQ, D % 2, s * P:(s + 1) * P]
                            for g in range(FT):
                                dh, dl = (v[:, ep, 2, g * P:(g + 1) * P] for v in (wThi, wTlo))
                                ah, al = (v[:, D % 2, g, toks] for v in (ahi, alo))
                                mm(out, ah, dh, start=(g == 0), stop=False)
                                mm(out, ah, dl, start=False, stop=False)
                                last = mm(out, al, dh, start=False, stop=(g == FT - 1))
                            if s == GROUP - 1:
                                last.then_inc(S["down_ready"], 1)
                    if J < CHUNKS and J % 4:
                        ep, k = J // 4, J % 4 - 1
                        turn_weights(1 - ep, k, i * 6 + 3 * (ep + 1) + k, (i + 1 + ep) * 48)
            glue_transposes(5)
            pe.wait_ge(S["glue_T_done"], 6 * GLUE)
            token_matmul(WsmT[:, 2, :])

        @block.scalar
        def _(act):
            fn = nc.scalar.activation
            act.sem_inc(S["exp_done"], 2)
            act.sem_inc(S["z_scaled"], 1)
            act.wait_ge(S["params_in"], 16 * PARAMS)
            fn(gt[:, :], gin[:, :], ACT.Tanh).then_inc(S["gates_tanh"], 1)
            act.wait_ge(S["gates_tanh"], 1)
            for n, group in enumerate(FOLD):
                act.wait_ge(S["fold_ready"], n + 1)
                _, dst, scale, _ = group
                src = score[:, n % 4, :].rearrange("p (s c) -> p s c", c=P)
                fn(dst, src, ACT.Copy, scale=scale).then_inc(S["fold_done"], 1)
            act.wait_ge(S["small_ready"], 1)
            fn(WsmT[:, 0:3, :], side[:, 0:3 * P].rearrange("p (s c) -> p s c", c=P), ACT.Copy)
            fn(WsmT[:, 3, 0:E], side[:, 3 * P:3 * P + E], ACT.Copy).then_inc(S["small_done"], 1)
            for s in range(2):
                act.wait_ge(S["small_ready"], 2 + s)
                fn(Wf[:, s, :], side[:, 0:P], ACT.Copy).then_inc(S["small_done"], 1)

            def glue_copies(n):
                for k in range(GLUE):
                    act.wait_ge(S["glue_T_ready"], n * GLUE + k + 1)
                    fn(xqT[:, qcols(k)], score[:, k, 0:GROUP * NQ], ACT.Copy).then_inc(S["glue_T_done"], 1)

            glue_copies(0)
            act.wait_ge(S["glue_T_done"], GLUE)

            def attention(L):
                def split_hi(kind, par, k, value):
                    act.wait_ge(S["piece_ready"], value)
                    if kind == "Q":
                        fn(QThi[:, par, qcols(k)], side[:, 0:GROUP * NQ], ACT.Copy).then_inc(S["piece_hi"], 1)
                    else:
                        cols = slice(k * GROUP * P, (k + 1) * GROUP * P)
                        fn(XThi[:, par, cols], side[:, :], ACT.Copy).then_inc(S["piece_hi"], 1)

                def values_hi(i, ahead, bq):
                    par = ahead % 2
                    if L.lat:
                        act.wait_ge(S["normed"], prepared(L, i, ahead))
                        fn(Xhi[:NQ, par, KT, :], xq[:NQ, bass.ds(bq, 1), :].rearrange("p a c -> p (a c)"), ACT.Copy)
                        fn(XThi[:, par, LATC], xqT[:, bass.ds(bq * NQ, NQ)], ACT.Copy)
                    else:
                        act.wait_ge(S[f"ctx_in{par}"], loaded(L, i, ahead))
                    fn(Xhi[:, par, 0:KT, :], raw[:, par, :, :], ACT.Copy).then_inc(S["values_hi"], 1)

                act.wait_ge(S["zeros_ready"], 1)
                for m, (kind, par, k) in enumerate(L.prologue):
                    if m == L.qgroups:
                        values_hi(0, 0, 0)
                    split_hi(kind, par, k, every.prologue(L, m) + 1)
                with act.Fori(0, LOOPS) as i:
                    m = 0
                    for n in range(L.N + 2):
                        q = (n - 1) % 2
                        if 1 <= n <= L.N:
                            for k in range(L.groups):
                                act.wait_ge(S["turned"], turned_c.at(L, i, n - 1, L.N, k + 1))
                                if k == 0:
                                    act.wait_ge(S["v_ready"], v_c.at(L, i, n - 1, L.N, -1))
                                w = min(GROUP, L.KT - k * GROUP) * P
                                G = (n - 1) * L.groups + k
                                fn(PThi[:, q, k * GROUP * P:k * GROUP * P + w], turn[:, G % 2, 0:w],
                                   ACT.Copy).then_inc(S["pt_hi"], 1)
                        if n < L.N:
                            p = n % 2
                            act.wait_ge(S["negm_ready"], tile_c.at(L, i, n, L.N, 1))
                            bias = negm[:, p:p + 1]
                            fn(prob[:, p, 0:2 * CH].rearrange("p (b c) -> p b c", b=2), score[:, 0:2, 0:CH], ACT.Exp,
                               bias=bias, accum_out=lsum[:, p, 0:1]).then_inc(S["exp_done"], 1)
                            last = fn(prob[:, p, 2 * CH:NK].rearrange("p (b c) -> p b c", b=2), score[:, 2:4, 0:CH],
                                      ACT.Exp, bias=bias, accum_out=lsum[:, p, 1:2])
                            if L.lat:
                                last = fn(prob[:, p, LATC], score[:, 3, CH:CH + NQ], ACT.Exp, bias=bias,
                                          accum_out=lsum[:, p, 2:3])
                            last.then_inc(S["exp_done"], 1)
                        if 1 <= n <= L.N:
                            act.wait_ge(S["v_ready"], v_c.at(L, i, n - 1, L.N, 1))
                            act.wait_ge(S["rinv_ready"], tile_c.at(L, i, n - 1, L.N, 1))
                            fn(Zs[:, q, :], vbank[:, 0:C], ACT.Copy, scale=rinv[:, q:q + 1]).then_inc(S["z_scaled"], 1)
                        if n < L.N and n % L.T == L.values_at:
                            ahead = n // L.T + 1
                            values_hi(i, ahead, 2 * i + ahead)
                        for kind, par, k in L.sched[n]:
                            if kind in "QX":
                                split_hi(kind, par, k, every.at(L, i, m) + 1)
                            m += 1

            attention(L0)
            glue_copies(1)
            for k in range(GLUE):
                act.wait_ge(S["ffn_biased"], k + 1)
                fn(tmp[:NQ, k * GROUP:(k + 1) * GROUP, :], tmp[:NQ, k * GROUP:(k + 1) * GROUP, :],
                   ACT.Tanh).then_inc(S["ffn_tanh"], 1)
            glue_copies(2)
            attention(L1)
            glue_copies(3)
            glue_copies(4)
            act.wait_ge(S["glue_T_done"], 5 * GLUE)
            fn(hThi[:, 0:B * NQ], xqT[:, 0:B * NQ], ACT.Copy).then_inc(S["h_hi"], 1)
            act.wait_ge(S["route_ready"], 1)
            fn(route[:NQ, 5, :], route[:NQ, 4, :], ACT.Exp).then_inc(S["route_exp"], 1)

            def weights_hi(ep, k, value):
                act.wait_ge(S["w_turned"], value)
                fn(wThi[:, ep, k, :], side[:, :], ACT.Copy, scale=WSCALE).then_inc(S["w_hi"], 1)

            for k in range(3):
                weights_hi(0, k, k + 1)
            with act.Fori(0, E // 2) as i:
                for J in range(CHUNKS + 1):
                    for f in range(FT):
                        if J < CHUNKS:
                            u = J * FT + f
                            act.wait_ge(S["gu_ready"], i * UNITS + u + 1)
                            fn(sil[:, u % 2, :], score[:, (u % 2) * 2, 0:4 * NQ], ACT.Silu,
                               scale=1.0 / WSCALE).then_inc(S["sil_ready"], 1)
                    if J >= 1:
                        D = J - 1
                        act.wait_ge(S["down_ready"], i * CHUNKS + D + 3)
                        for s in range(GROUP):
                            last = fn(sqs[:NQ, D % 2, s, :], turn[:NQ, D % 2, s * P:(s + 1) * P], ACT.Square,
                                      scale=1.0 / WSCALE ** 2, accum_out=ssq[:NQ, D % 2, s:s + 1])
                        last.then_inc(S["sq_ready"], 1)
                    if J < CHUNKS and J % 4:
                        ep, k = J // 4, J % 4 - 1
                        weights_hi(1 - ep, k, i * 6 + 3 * (ep + 1) + k + 1)
            glue_copies(5)

        @block.vector
        def _(dve):
            v = nc.vector
            chain, norms = [0], [0]

            def link(ins):
                chain[0] += 1
                ins.then_inc(S["dve_chain"], 1)
                dve.wait_ge(S["dve_chain"], chain[0])

            dve.sem_inc(S["pt_lo"], 2)
            dve.sem_inc(S["act_ready"], 2)
            dve.sem_inc(S["acc_ready"], 2)

            def wide(stat):
                return stat.unsqueeze(2).to_broadcast([NQ, B, C])

            def over(vec):
                return vec.unsqueeze(1).to_broadcast([NQ, B, C])

            def norm(src, dst, eps, mean=True, ready=None):
                s0, s1, s2 = (small[:NQ, k, :] for k in range(3))
                if mean:
                    link(v.reduce_sum(s0, src, AX.X))
                    link(v.tensor_scalar(s1, s0, 1.0 / C, None, ALU.mult))
                    link(v.tensor_tensor(dst, src, wide(s1), ALU.subtract))
                    src = dst
                link(v.tensor_tensor(tmp[:NQ, :, :], src, src, ALU.mult))
                link(v.reduce_sum(s0, tmp[:NQ, :, :], AX.X))
                v.tensor_scalar(s1, s0, 1.0 / C, eps, ALU.mult, ALU.add).then_inc(S["var_ready"], 1)
                norms[0] += 1
                dve.wait_ge(S["rstd_ready"], norms[0])
                last = v.tensor_tensor(dst, src, wide(s2), ALU.mult)
                link(last) if ready is None else last.then_inc(ready, 1)

            xv, xn = x[:NQ, :, :], xq[:NQ, 0:B, :]
            dve.wait_ge(S["zeros_ready"], 1)
            dve.wait_ge(S["x_in"], 16)
            norm(xv, xn, LN_EPS)
            norm(xn, xn, LN_EPS)
            dve.wait_ge(S["params_in"], 16 * PARAMS)
            link(v.tensor_tensor(xn, xn, over(lnlw[:NQ, :]), ALU.mult))
            v.tensor_tensor(xn, xn, over(lnlb[:NQ, :]), ALU.add).then_inc(S["xq_ready"], 1)
            dve.wait_ge(S["gates_tanh"], 1)
            link(v.tensor_scalar(obias[:, :], obias[:, :], gt[:, 1:2], None, ALU.mult))

            def attention(L):
                def stats(i, ahead):
                    par, done = ahead % 2, prepared(L, i, ahead)
                    dve.wait_ge(S[f"ctx_in{par}"], loaded(L, i, ahead))
                    for t in range(KT):
                        last = v.bn_stats(stat6[:, t, :], raw[:, par, t, :])
                    last.then_inc(S["stat_step"], 1)
                    dve.wait_ge(S["stat_step"], prepared(L, i, ahead, 2) - 1)
                    dve.sem_inc(S["waited"], 1)
                    for t in range(KT):
                        last = v.bn_aggr(mv[:, t, :], stat6[:, t, :])
                    last.then_inc(S["stat_step"], 1)
                    dve.wait_ge(S["stat_step"], prepared(L, i, ahead, 2))
                    dve.wait_ge(S["normed"], done - 1)
                    v.tensor_scalar(nmean_k[:, :], mv[:, :, 0], -1.0, None, ALU.mult)
                    v.tensor_scalar(var_k[:, :], mv[:, :, 1], LN_EPS, None, ALU.add).then_inc(S["stats_ready"], 1)

                def split_lo(kind, par, k, value):
                    dve.wait_ge(S["piece_hi"], value)
                    if kind == "Q":
                        v.tensor_tensor(QTlo[:, par, qcols(k)], side[:, 0:GROUP * NQ], QThi[:, par, qcols(k)],
                                        ALU.subtract).then_inc(S["piece_done"], 1)
                    else:
                        cols = slice(k * GROUP * P, (k + 1) * GROUP * P)
                        v.tensor_tensor(XTlo[:, par, cols], side[:, :], XThi[:, par, cols],
                                        ALU.subtract).then_inc(S["piece_done"], 1)

                if L.lat:
                    stats(0, 0)
                for m, (kind, par, k) in enumerate(L.prologue):
                    split_lo(kind, par, k, split.prologue(L, m) + 1)
                with dve.Fori(0, LOOPS) as i:
                    m = 0
                    for n in range(L.N + 2):
                        q, p = (n - 1) % 2, n % 2
                        if L.lat and n < L.N and n % L.T == 0:
                            stats(i, n // L.T + 1)
                        if 1 <= n <= L.N:
                            dve.wait_ge(S["exp_done"], exp_c.at(L, i, n - 1, L.N, 2))
                            v.reduce_sum(lall[:, q:q + 1], lsum[:, q, 0:L.sums], AX.X).then_inc(S["sum_ready"], 1)
                            dve.wait_ge(S["sum_ready"], tile_c.at(L, i, n - 1, L.N, 1))
                            v.reciprocal(rinv[:, q:q + 1], lall[:, q:q + 1]).then_inc(S["rinv_ready"], 1)
                            for k in range(L.groups):
                                dve.wait_ge(S["pt_hi"], pthi_c.at(L, i, n - 1, L.N, k + 1))
                                w = min(GROUP, L.KT - k * GROUP) * P
                                cols = slice(k * GROUP * P, k * GROUP * P + w)
                                G = (n - 1) * L.groups + k
                                v.tensor_tensor(PTlo[:, q, cols], turn[:, G % 2, 0:w], PThi[:, q, cols],
                                                ALU.subtract).then_inc(S["pt_lo"], 1)
                        if n < L.N:
                            dve.wait_ge(S["score_ready"], score_c.at(L, i, n, L.N, 1))
                            v.reduce_max(mx[:, p, 0:1], score[:, 0:2, 0:CH], AX.XY)
                            dve.wait_ge(S["score_ready"], score_c.at(L, i, n, L.N, 2))
                            if L.lat:
                                v.reduce_max(mx[:, p, 1:2], score[:, 2, 0:CH], AX.X)
                                last = v.reduce_max(mx[:, p, 2:3], score[:, 3, 0:CH + NQ], AX.X)
                            else:
                                last = v.reduce_max(mx[:, p, 1:2], score[:, 2:4, 0:CH], AX.XY)
                            last.then_inc(S["max_part"], 1)
                            dve.wait_ge(S["max_part"], tile_c.at(L, i, n, L.N, 1))
                            v.reduce_max(negm[:, p:p + 1], mx[:, p, 0:L.maxes], AX.X,
                                         negate=True).then_inc(S["negm_ready"], 1)
                        for kind, par, k in L.sched[n]:
                            if kind in "QX":
                                split_lo(kind, par, k, split.at(L, i, m) + 1)
                            elif kind == "Z":
                                dve.wait_ge(S["piece_ready"], every.at(L, i, m) + 1)
                                zp = k // L.T
                                c0 = (k % L.T) * P
                                v.tensor_copy(ZT[:, zp, c0:c0 + P], side[:, 0:P]).then_inc(S["piece_done"], 1)
                            else:
                                dve.wait_ge(S["piece_ready"], every.at(L, i, m) + 1)
                                xb = x[:NQ, bass.ds(2 * i + par, 1), :].rearrange("p a c -> p (a c)")
                                v.tensor_tensor(xb, side[:NQ, 0:C], xb, ALU.add).then_inc(S["piece_done"], 1)
                            m += 1

            attention(L0)
            dve.wait_ge(S["piece_done"], every.at(L0, LOOPS - 1, L0.pieces))
            dve.wait_ge(S["values_done"], prepared(L0, LOOPS - 1, 2))
            norm(xv, xn, LN_EPS, ready=S["xq_ready"])
            for k in range(GLUE):
                part = tmp[:NQ, k * GROUP:(k + 1) * GROUP, :]
                dve.wait_ge(S["token_mm"], k + 1)
                ps = score[:NQ, k, :].rearrange("p (s c) -> p s c", c=C)
                v.tensor_tensor(part, ps, fbias[:NQ, :].unsqueeze(1).to_broadcast([NQ, GROUP, C]),
                                ALU.add).then_inc(S["ffn_biased"], 1)
            for k in range(GLUE):
                part = tmp[:NQ, k * GROUP:(k + 1) * GROUP, :]
                xk = x[:NQ, k * GROUP:(k + 1) * GROUP, :]
                dve.wait_ge(S["ffn_tanh"], k + 1)
                link(v.scalar_tensor_tensor(out=xk, in0=part, scalar=gt[:NQ, 2:3], in1=xk, op0=ALU.mult, op1=ALU.add))
            norm(xv, xn, LN_EPS, ready=S["xq_ready"])
            link(v.tensor_tensor(xv, xv, over(obias[:NQ, :]), ALU.add))
            attention(L1)
            dve.wait_ge(S["piece_done"], every.at(L1, LOOPS - 1, L1.pieces))
            norm(xv, xn, LN_EPS, ready=S["xq_ready"])
            for k in range(GLUE):
                dve.wait_ge(S["token_mm"], GLUE + k + 1)
                link(v.tensor_copy(xq[:NQ, k * GROUP:(k + 1) * GROUP, :],
                                   score[:NQ, k, :].rearrange("p (s c) -> p s c", c=C)))
            norm(xn, xn, RMS_EPS, mean=False)
            v.tensor_tensor(xn, xn, over(innw[:NQ, :]), ALU.mult).then_inc(S["xq_ready"], 1)
            dve.wait_ge(S["h_hi"], 1)
            v.tensor_tensor(hTlo[:, 0:B * NQ], xqT[:, 0:B * NQ], hThi[:, 0:B * NQ], ALU.subtract).then_inc(S["h_split"], 1)

            R = [route[:NQ, k, :].rearrange("p (b e) -> p b e", e=E) for k in range(8)]
            st = [small[:NQ, k, :] for k in range(8)]

            def each(s):
                return s.unsqueeze(2).to_broadcast([NQ, B, E])

            io = iota8[:NQ, :].unsqueeze(1).to_broadcast([NQ, B, E])
            dve.wait_ge(S["logits_ready"], 1)
            link(v.tensor_copy(R[0], vbank[:NQ, 0:B * E].rearrange("p (b e) -> p b e", e=E)))
            link(v.tensor_tensor(R[1], R[0], ebias[:NQ, :].unsqueeze(1).to_broadcast([NQ, B, E]), ALU.add))
            for pick in (2, 3):
                link(v.reduce_max(st[0], R[1], AX.X))
                link(v.tensor_tensor(R[6], R[1], each(st[0]), ALU.is_equal))
                link(v.tensor_tensor(R[7], R[6], io, ALU.mult))
                link(v.tensor_reduce(st[1], R[7], AX.X, ALU.min))
                link(v.tensor_tensor(R[pick], io, each(st[1]), ALU.is_equal))
                link(v.scalar_tensor_tensor(out=R[1], in0=R[pick], scalar=-3.0e38, in1=R[1], op0=ALU.mult, op1=ALU.add))
            link(v.tensor_tensor(R[2], R[2], R[3], ALU.add))
            link(v.tensor_scalar(R[3], R[2], -1.0, 3.0e38, ALU.add, ALU.mult))
            link(v.tensor_tensor(R[3], R[3], R[0], ALU.add))
            link(v.reduce_max(st[0], R[3], AX.X))
            link(v.tensor_tensor(R[6], R[0], each(st[0]), ALU.subtract))
            link(v.tensor_tensor(R[6], R[6], R[2], ALU.mult))
            v.tensor_copy(R[4], R[6]).then_inc(S["route_ready"], 1)
            dve.wait_ge(S["route_exp"], 1)
            link(v.tensor_tensor(R[5], R[5], R[2], ALU.mult))
            link(v.reduce_sum(st[0], R[5], AX.X))
            link(v.reciprocal(st[1], st[0]))
            link(v.tensor_tensor(R[0], R[5], each(st[1]), ALU.mult))
            link(v.memset(tmp[:NQ, :, :], 0.0))

            def weights_lo(ep, k, value):
                dve.wait_ge(S["w_hi"], value)
                v.scalar_tensor_tensor(out=wTlo[:, ep, k, :], in0=side[:, :], scalar=WSCALE, in1=wThi[:, ep, k, :],
                                       op0=ALU.mult, op1=ALU.subtract).then_inc(S["w_lo"], 1)

            for k in range(3):
                weights_lo(0, k, k + 1)
            with dve.Fori(0, E // 2) as i:
                for J in range(CHUNKS + 1):
                    for f in range(FT):
                        if J < CHUNKS:
                            u = J * FT + f
                            dve.wait_ge(S["sil_ready"], i * UNITS + u + 1)
                            dve.wait_ge(S["alo_ready"], i * UNITS + max(u, 1))
                            v.tensor_tensor(actf[:, u % 2, :], score[:, (u % 2) * 2 + 1, 0:4 * NQ], sil[:, u % 2, :],
                                            ALU.mult).then_inc(S["act_ready"], 1)
                            dve.wait_ge(S["act_ready"], i * UNITS + u + 3)
                            if f == 0:
                                dve.wait_ge(S["down_ready"], i * CHUNKS + J + 1)
                            v.tensor_copy(ahi[:, J % 2, f, :], actf[:, u % 2, :]).then_inc(S["ahi_ready"], 1)
                    if J >= 1:
                        D, j = J - 1, (J - 1) % 4
                        e = 2 * i + D // 4
                        d = D % 2
                        base = i * (2 * CHUNKS) + 2 * D
                        dve.wait_ge(S["sq_ready"], i * CHUNKS + D + 1)
                        v.tensor_scalar(coef[:NQ, d, 0, :], ssq[:NQ, d, :], 1.0 / C, RMS_EPS, ALU.mult,
                                        ALU.add).then_inc(S["ms_ready"], 1)
                        dve.wait_ge(S["coef_ready"], i * CHUNKS + D + 1)
                        gate = route[:NQ, 0, :].rearrange("p (b e) -> p b e", e=E)[:, j * 4:(j + 1) * 4, bass.ds(e, 1)]
                        v.scalar_tensor_tensor(out=coef[:NQ, d, 2, :].unsqueeze(2), in0=coef[:NQ, d, 1, :].unsqueeze(2),
                                               scalar=1.0 / WSCALE ** 2, in1=gate, op0=ALU.mult,
                                               op1=ALU.mult).then_inc(S["coef_step"], 1)
                        dve.wait_ge(S["coef_step"], base + 1)
                        for s in range(GROUP):
                            last = v.scalar_tensor_tensor(
                                out=term[:NQ, d, s, :], in0=turn[:NQ, d, s * P:(s + 1) * P],
                                scalar=coef[:NQ, d, 2, s:s + 1],
                                in1=enw[:NQ, bass.ds(e, 1), :].rearrange("p a c -> p (a c)"),
                                op0=ALU.mult, op1=ALU.mult)
                        last.then_inc(S["coef_step"], 1)
                        dve.wait_ge(S["coef_step"], base + 2)
                        v.tensor_tensor(tmp[:NQ, j * 4:(j + 1) * 4, :], tmp[:NQ, j * 4:(j + 1) * 4, :],
                                        term[:NQ, d, :, :], ALU.add).then_inc(S["acc_ready"], 1)
                    if J < CHUNKS and J % 4:
                        ep, k = J // 4, J % 4 - 1
                        weights_lo(1 - ep, k, i * 6 + 3 * (ep + 1) + k + 1)
            dve.wait_ge(S["acc_ready"], E // 2 * CHUNKS + 2)
            link(v.tensor_copy(xn, tmp[:NQ, :, :]))
            norm(xn, xn, RMS_EPS, mean=False)
            v.tensor_tensor(xn, xn, over(outnw[:NQ, :]), ALU.mult).then_inc(S["xq_ready"], 1)
            for k in range(GLUE):
                dve.wait_ge(S["token_mm"], 2 * GLUE + k + 1)
                xk = x[:NQ, k * GROUP:(k + 1) * GROUP, :]
                last = v.scalar_tensor_tensor(out=xk, in0=score[:NQ, k, :].rearrange("p (s c) -> p s c", c=C),
                                              scalar=gt[:NQ, 3:4], in1=xk, op0=ALU.mult, op1=ALU.add)
            last.then_inc(S["x_final"], 1)


_INS = ['x', 'ctx_1024', 'g_xattn', 'g_ffn', 'L0_xattn_ln_m_w', 'L0_xattn_ln_m_b', 'L0_xattn_ln_l_w',
        'L0_xattn_ln_l_b', 'L0_xattn_Wq', 'L0_xattn_Wkv', 'L0_xattn_Wout', 'L0_ffn_weight', 'L0_ffn_aux_weight1',
        'L0_ffn_aux_weight2', 'L0_ffn_bias', 'L1_xattn_Wq', 'L1_xattn_Wk', 'L1_xattn_Wv', 'L1_xattn_Wo',
        'L1_xattn_bo', 'L1_ffn_W_in', 'L1_ffn_in_norm_w', 'L1_ffn_Wr', 'L1_ffn_expert_bias', 'L1_ffn_Wg',
        'L1_ffn_Wu', 'L1_ffn_Wd', 'L1_ffn_enorm_w', 'L1_ffn_out_norm_w', 'L1_ffn_W_out']
_OUTS = [((B, NQ, C), 'float32')]


def kernel(**inputs):
    import numpy as _np
    import concourse.bacc as _bacc
    from concourse import mybir as _mybir
    from concourse.bass_utils import run_bass_kernel_spmd as _run

    nc = _bacc.Bacc("TRN2", target_bir_lowering=False, num_devices=1)
    arrays, args = {}, {}
    for name in _INS:
        a = _np.ascontiguousarray(inputs[name])
        arrays[f"in_{name}_dram"] = a
        args[name] = nc.dram_tensor(f"in_{name}_dram", a.shape, _mybir.dt.from_np(a.dtype), kind="ExternalInput").ap()
    for i, (shape, dtype) in enumerate(_OUTS):
        dt = _mybir.dt.from_np(_np.dtype(dtype))
        args["out"] = nc.dram_tensor(f"out_{i}_dram", shape, dt, kind="ExternalOutput").ap()
    flamingo_kernel(nc, args)
    r = _run(nc, [arrays], core_ids=[0])
    return r.results[0]["out_0_dram"]
```

```python
from contextlib import ExitStack

import concourse.bass as bass
from concourse import mybir

F32 = mybir.dt.float32
F16 = mybir.dt.float16
ALU = mybir.AluOpType
ACT = mybir.ActivationFunctionType
AX = mybir.AxisListType

P = 128
B, NQ, C = 16, 100, 128
NK = 1444
KT = (NK + P - 1) // P
KLAST = NK - (KT - 1) * P
CH = NK // 4
DH = 64
LN_EPS = 1e-5
RMS_EPS = 1.1920928955078125e-07
E, FF = 8, 512
FT = FF // P
WSCALE = 256.0
GROUP = 4


class Layer:

    def __init__(self, index, heads, with_latents):
        self.index = index
        self.heads = heads
        self.lat = with_latents
        self.T = (heads * NQ + P - 1) // P
        self.N = 2 * self.T
        self.KT = KT + (1 if with_latents else 0)
        self.groups = (self.KT + GROUP - 1) // GROUP
        self.qgroups = heads // GROUP
        self.early = 3
        self.maxes = 3 if with_latents else 2
        self.sums = 2 if with_latents else 1
        self.values_at = 4 if with_latents else 2
        first_q, first_x = (1, 4) if with_latents else (4, 8)
        self.sched = [[] for _ in range(self.N + 3)]
        for n in range(self.N + 3):
            self.sched[n].append(("Z", 0 if 3 <= n < self.T + 3 else 1, (n - 3) % self.T))
            if n % self.T == 3 and n < self.N:
                self.sched[n].append(("O", 1 - n // self.T, n // self.T))
            if n < self.N:
                t, into = n % self.T, 1 - n // self.T
                if first_q <= t < first_q + self.qgroups:
                    self.sched[n].append(("Q", into, t - first_q))
                if first_x <= t < first_x + 3:
                    self.sched[n].append(("X", into, t - first_x))
        self.sched[self.N + 2].append(("O", 1, 2))
        self.prologue = [("Q", 0, k) for k in range(self.qgroups)] + [("X", 0, k) for k in range(3)]
        self.flat = [s for step in self.sched[:self.N] for s in step]
        self.tail = [s for step in self.sched[self.N:] for s in step]


L0 = Layer(0, 8, True)
L1 = Layer(1, 16, False)
LOOPS = B // 2


class Count:

    def __init__(self, per0, per1, extra=0, credit=0):
        self.per = (per0, per1)
        self.base = (credit, credit + per0 * (LOOPS * L0.N + extra))

    def at(self, layer, i, n, k=0):
        per = self.per[layer.index]
        return i * (per * layer.N) + (self.base[layer.index] + per * n + k)


def flamingo_kernel(nc, a):
    ctx = ExitStack()
    with ctx:
        def sb(name, shape, dt=F32):
            return ctx.enter_context(nc.sbuf_tensor(name, shape, dt))

        def sem(name):
            return ctx.enter_context(nc.semaphore(name))

        x = sb("x", [P, B + 1, C])
        xq = sb("xq", [P, B + 1, C])
        xqT = sb("xqT", [P, (B + 1) * NQ])
        tmp = sb("tmp", [P, B, C])
        raw = sb("raw", [P, 2, KT, C])
        Xhi = sb("Xhi", [P, 2, KT + 1, C], F16)
        Xlo = sb("Xlo", [P, 2, KT + 1, C], F16)
        KW = (KT + 1) * P
        XThi = sb("XThi", [P, 2, KW], F16)
        XTlo = sb("XTlo", [P, 2, KW], F16)
        QW = L1.T * P
        QThi = sb("QThi", [P, 2, QW], F16)
        QTlo = sb("QTlo", [P, 2, QW], F16)
        prob = sb("prob", [P, 2, KW])
        PThi = sb("PThi", [P, 2, KW], F16)
        PTlo = sb("PTlo", [P, 2, KW], F16)
        Zs = sb("Zs", [P, 2, C])
        ZT = sb("ZT", [P, 2, QW])
        Amat = sb("Amat", [P, L0.heads + L1.heads, C])
        Mmat = sb("Mmat", [P, L0.heads + L1.heads, C])
        ident = sb("ident", [P, P])
        mx = sb("mx", [P, 2, 4])
        negm = sb("negm", [P, 2])
        lsum = sb("lsum", [P, 2, 4])
        lall = sb("lall", [P, 2])
        rinv = sb("rinv", [P, 2])
        stat6 = sb("stat6", [P, KT, 6])
        mv = sb("mv", [P, KT, 2])
        rstd_k = sb("rstd_k", [P, KT])
        nmean_k = sb("nmean_k", [P, KT])
        lnmw = sb("lnmw", [P, C])
        lnmb = sb("lnmb", [P, C])
        lnlw = sb("lnlw", [P, C])
        lnlb = sb("lnlb", [P, C])
        fbias = sb("fbias", [P, C])
        obias = sb("obias", [P, C])
        innw = sb("innw", [P, C])
        outnw = sb("outnw", [P, C])
        enw = sb("enw", [P, E, C])
        ebias = sb("ebias", [P, E])
        gin = sb("gin", [P, 4])
        gt = sb("gt", [P, 4])
        small = sb("small", [P, 8, B])
        Wsm = sb("Wsm", [P, 6, C])
        WsmT = sb("WsmT", [P, 4, C])
        Wf = sb("Wf", [P, 2, C])
        route = sb("route", [P, 8, B * E])
        iota8 = sb("iota8", [P, E])
        var_k = sb("var_k", [P, KT])
        minus_half = sb("minus_half", [P, B])
        coef = sb("coef", [P, 2, 3, GROUP])
        ssq = sb("ssq", [P, 2, GROUP])
        hThi, hTlo = QThi[:, 0, :], QTlo[:, 0, :]
        wThi, wTlo = (w[:, :, 0:3 * FT * P].rearrange("p b (k f) -> p b k f", k=3) for w in (XThi, XTlo))
        ahi, alo = (w[:, :, 0:FT * 4 * NQ].rearrange("p b (f n) -> p b f n", f=FT) for w in (PThi, PTlo))
        sil, actf = prob[:, :, 0:4 * NQ], prob[:, :, 4 * NQ:8 * NQ]
        sqs, term, dsb = (ZT[:, :, s * 512:(s + 1) * 512].rearrange("p b (s c) -> p b s c", c=C) for s in range(3))
        LATC = slice(KT * P, KT * P + NQ)

        wraw = sb("wraw", [P, 48, C])
        wT = sb("wT", [P, 20, C])

        score = ctx.enter_context(nc.psum_tensor("score", [P, 4, 512], F32))
        turn = ctx.enter_context(nc.psum_tensor("turn", [P, 2, 512], F32))
        vbank = ctx.enter_context(nc.psum_tensor("vbank", [P, 512], F32))
        side = ctx.enter_context(nc.psum_tensor("side", [P, 512], F32))

        S = {n: sem(n) for n in """waited down_copied null_ready score_copied var_ready rstd_ready ms_ready coef_ready acc_ready act_ready ahi_ready alo_ready coef_step ctx_in0 ctx_in1 down_ready dve_chain
            exp_done ffn_biased ffn_tanh fold_done fold_ready gates_tanh glue_T_done
            glue_T_ready gu_ready h_hi h_split ident_ready logits_ready max_part moe_in0
            moe_in1 negm_ready normed out_in params_in piece_done piece_hi piece_ready
            pt_hi pt_lo rinv_ready route_exp route_ready scaled score_ready sil_ready
            small_done small_ready sq_ready stat_step stats_ready sum_ready token_mm
            turned v_ready values_done values_hi w_hi w_lo w_turned weights_in x_final
            x_in xq_ready z_scaled zeros_ready""".split()}

        score_c = Count(2, 2)
        copied_c = Count(2, 2, credit=2)
        negm_c = Count(1, 1)
        exp_c = Count(1, 1, credit=1)
        turned_c = Count(L0.groups, L1.groups, extra=1)
        pthi_c = Count(L0.groups, L1.groups, extra=1)
        ptlo_c = Count(L0.groups, L1.groups, extra=1, credit=2)
        rinv_c = Count(1, 1, extra=1, credit=1)
        v_c = Count(1, 1, extra=2, credit=1)
        z_c = Count(1, 1, extra=2, credit=1)

        class PieceCount:

            def __init__(self, kinds):
                def n(seq):
                    return sum(s[0] in kinds for s in seq)
                self.kinds = kinds
                self.loop = (n(L0.flat), n(L1.flat))
                self.pro = (n(L0.prologue), n(L1.prologue))
                self.start = (0, self.pro[0] + LOOPS * self.loop[0] + n(L0.tail))

            def prologue(self, layer, m):
                return self.start[layer.index] + sum(s[0] in self.kinds for s in layer.prologue[:m])

            def at(self, layer, i, m):
                done = sum(s[0] in self.kinds for s in (layer.flat + layer.tail)[:m])
                return i * self.loop[layer.index] + (self.start[layer.index] + self.pro[layer.index] + done)

        every = PieceCount("ZOQX")
        split = PieceCount("QX")

        def operands_complete(layer, par):
            last = [m for m, s in enumerate(layer.flat) if s[0] in "QX" and s[1] == par]
            return max(last) + 1

        PREPARED = B + 1

        def prepared(layer, i, ahead, per=1):
            return i * (2 * per) + (PREPARED * layer.index + ahead + 1) * per

        def loaded(layer, i, ahead):
            if ahead % 2:
                return i * 32 + (LOOPS * layer.index + 1) * 32
            return i * 32 + ((LOOPS + 1) * layer.index + ahead // 2 + 1) * 32

        GLUE = B // GROUP
        CHUNKS, UNITS = 8, 8 * FT
        PARAMS, WEIGHTS = 12, 13

        def half(block, h):
            return block[(h % 2) * DH:(h % 2 + 1) * DH, :]

        def fold_groups():
            def turns(src, dst):
                return (0, wT[:, dst:dst + 4, :], 1.0, [(wraw[:, src + s, :], None) for s in range(4)])
            out = [turns(0, 0), turns(4, 4), turns(8, 8), turns(40, 12), turns(44, 16)]
            for L, lq, lk, lv, lo in ((L0, (wT, 0), (wT, 4), (wT, 8), (wraw, 12)),
                                      (L1, (wraw, 16), (wraw, 24), (wraw, 32), (wT, 12))):
                first = L0.heads * L.index
                for dst, l, r, need, scale in ((Amat, lq, lk, 2, DH ** -0.5),
                                               (Mmat, lv, lo, 5, gt[:, L.index:L.index + 1])):
                    for h0 in [g * 8 + par for g in range(L.heads // 8) for par in range(2)]:
                        out.append((need, dst[:, first + h0:first + h0 + 7:2, :], scale,
                                    [(half(l[0][:, l[1] + h // 2, :], h), half(r[0][:, r[1] + h // 2, :], h))
                                     for h in range(h0, h0 + 8, 2)]))
            return out

        FOLD = fold_groups()
        FOLDS = len(FOLD)

        def qcols(k):
            return slice(k * GROUP * NQ, (k + 1) * GROUP * NQ)

        block = ctx.enter_context(nc.Block())

        @block.sync
        def _(sp):
            def row(v):
                return v.rearrange("(a c) -> a c", a=1)

            sp.dma_start(x[:NQ, 1:, :], a["x"].rearrange("b q c -> q b c")).then_inc(S["x_in"], 16)
            for dst, src in ((lnlw, "L0_xattn_ln_l_w"), (lnlb, "L0_xattn_ln_l_b"), (lnmw, "L0_xattn_ln_m_w"),
                             (lnmb, "L0_xattn_ln_m_b"), (fbias, "L0_ffn_bias"), (obias, "L1_xattn_bo"),
                             (innw, "L1_ffn_in_norm_w"), (outnw, "L1_ffn_out_norm_w"),
                             (ebias, "L1_ffn_expert_bias")):
                sp.dma_start(dst[:, :], row(a[src]).to_broadcast([P, dst.shape[1]])).then_inc(S["params_in"], 16)
            sp.dma_start(gin[:, 0:2], row(a["g_xattn"]).to_broadcast([P, 2])).then_inc(S["params_in"], 16)
            sp.dma_start(gin[:, 2:4], row(a["g_ffn"]).to_broadcast([P, 2])).then_inc(S["params_in"], 16)
            sp.dma_start(enw[:, :, :], a["L1_ffn_enorm_w"].rearrange("(a e) d -> a e d", a=1)
                         .to_broadcast([P, E, C])).then_inc(S["params_in"], 16)
            for at, n, src in ((0, 4, a["L0_xattn_Wq"].rearrange("c (k e) -> c k e", e=P)),
                               (4, 8, a["L0_xattn_Wkv"].rearrange("c (k e) -> c k e", e=P)),
                               (12, 4, a["L0_xattn_Wout"].rearrange("(k e) c -> e k c", e=P)),
                               (16, 8, a["L1_xattn_Wq"].rearrange("(k e) c -> e k c", e=P)),
                               (24, 8, a["L1_xattn_Wk"].rearrange("(k e) c -> e k c", e=P)),
                               (32, 8, a["L1_xattn_Wv"].rearrange("(k e) c -> e k c", e=P)),
                               (40, 8, a["L1_xattn_Wo"].rearrange("c (k e) -> c k e", e=P))):
                sp.dma_start(wraw[:, at:at + n, :], src).then_inc(S["weights_in"], 16)
            for s, w in enumerate(("L0_ffn_weight", "L0_ffn_aux_weight1", "L0_ffn_aux_weight2",
                                   "L1_ffn_W_in", "L1_ffn_W_out")):
                sp.dma_start(Wsm[:, s, :], a[w]).then_inc(S["weights_in"], 16)
            sp.dma_start(Wsm[0:E, 5, :], a["L1_ffn_Wr"]).then_inc(S["weights_in"], 16)

            def load(src, par):
                full = src[0:(KT - 1) * P, :].rearrange("(t p) c -> p t c", p=P)
                sp.dma_start(raw[:, par, 0:KT - 1, :], full).then_inc(S[f"ctx_in{par}"], 16)
                sp.dma_start(raw[:KLAST, par, KT - 1, :], src[(KT - 1) * P:NK, :]).then_inc(S[f"ctx_in{par}"], 16)

            c = a["ctx_1024"]
            sp.wait_ge(S["zeros_ready"], 1)
            for L in (L0, L1):
                if L is L1:
                    sp.wait_ge(S["values_done"], prepared(L0, LOOPS - 1, 2))
                    sp.wait_ge(S["piece_done"], every.at(L0, LOOPS - 1, len(L0.flat + L0.tail)))
                load(c[0], 0)
                load(c[1], 1)
                with sp.Fori(0, LOOPS - 1) as i:
                    for par in range(2):
                        sp.wait_ge(S["values_done"], prepared(L, i, par))
                        sp.sem_inc(S["waited"], 1)
                        m = operands_complete(L, 1) if par else 0
                        sp.wait_ge(S["piece_done"], every.at(L, i, m))
                        sp.sem_inc(S["waited"], 1)
                        load(c[bass.ds(2 * i + 2 + par, 1), :, :].rearrange("a k c -> (a k) c"), par)
                sp.wait_ge(S["values_done"], prepared(L, LOOPS - 1, 0))
                sp.wait_ge(S["piece_done"], every.at(L, LOOPS - 1, 0))
                load(c[0], 0)

            def load_expert(ep, e):
                for at, src in ((0, a["L1_ffn_Wg"][bass.ds(e, 1)].rearrange("a (k p) d -> p (a k) d", p=P)),
                                (4, a["L1_ffn_Wu"][bass.ds(e, 1)].rearrange("a (k p) d -> p (a k) d", p=P)),
                                (8, a["L1_ffn_Wd"][bass.ds(e, 1)].rearrange("a o (k p) -> o (a k) p", p=P))):
                    at += ep * 3 * FT
                    sp.dma_start(wraw[:, at:at + FT, :], src).then_inc(S[f"moe_in{ep}"], 16)

            sp.wait_ge(S["fold_done"], FOLDS)
            load_expert(0, 0)
            load_expert(1, 1)
            with sp.Fori(0, E // 2 - 1) as i:
                for ep in range(2):
                    sp.wait_ge(S["w_lo"], i * 6 + 3 * (ep + 1))
                    sp.sem_inc(S["waited"], 1)
                    load_expert(ep, 2 * i + 2 + ep)
            sp.wait_ge(S["w_lo"], 3 * (E - 1))
            load_expert(0, 0)
            sp.wait_ge(S["moe_in0"], 48 * (E // 2 + 1))
            sp.wait_ge(S["x_final"], 1)
            sp.dma_start(a["out"].rearrange("b q c -> q b c"), x[:NQ, 1:, :]).then_inc(S["out_in"], 16)
            sp.wait_ge(S["out_in"], 16)

        @block.gpsimd
        def _(pool):
            pool.sem_inc(S["alo_ready"], 1)
            nc.gpsimd.memset(ident[:, :], 0.0).then_inc(S["ident_ready"], 1)
            pool.wait_ge(S["ident_ready"], 1)
            nc.gpsimd.affine_select(out=ident[:, :], in_=ident[:, :], compare_op=ALU.not_equal, fill=1.0, base=0,
                                    pattern=[[-1, P]], channel_multiplier=1).then_inc(S["ident_ready"], 1)
            for par in range(2):
                nc.gpsimd.memset(raw[:, par, KT - 1, :], 0.0)
                nc.gpsimd.memset(Xhi[:, par, KT, :], 0.0)
                nc.gpsimd.memset(Xlo[:, par, KT, :], 0.0)
                nc.gpsimd.memset(prob[:, par, NK:KW], 0.0)
                nc.gpsimd.memset(QThi[:, par, :], 0.0)
                nc.gpsimd.memset(QTlo[:, par, :], 0.0)
            nc.gpsimd.memset(minus_half[:, :], -0.5)
            nc.gpsimd.memset(xq[:, B, :], 0.0)
            nc.gpsimd.memset(xqT[:, B * NQ:], 0.0)
            for e in range(E):
                last = nc.gpsimd.memset(iota8[:, e:e + 1], float(e - E))
            last.then_inc(S["zeros_ready"], 1)

            def prepare(L, i, ahead, bq):
                par = ahead % 2
                X = raw[:, par, :, :]
                done = prepared(L, i, ahead)
                if L.lat:
                    pool.wait_ge(S["stats_ready"], done)
                    nc.gpsimd.tensor_tensor(rstd_k[:, :], var_k[:, :], minus_half[:, 0:KT], ALU.pow).then_inc(S["scaled"], 1)
                    pool.wait_ge(S["scaled"], prepared(L, i, ahead, 3) - 2)
                    pool.sem_inc(S["waited"], 1)
                    for t in range(KT):
                        last = nc.gpsimd.tensor_scalar(raw[:, par, t, :], raw[:, par, t, :], nmean_k[:, t:t + 1],
                                                       rstd_k[:, t:t + 1], ALU.add, ALU.mult)
                    last.then_inc(S["scaled"], 1)
                    pool.wait_ge(S["scaled"], prepared(L, i, ahead, 3) - 1)
                    nc.gpsimd.tensor_tensor(X, X, lnmw[:, :].unsqueeze(1).to_broadcast([P, KT, C]),
                                            ALU.mult).then_inc(S["scaled"], 1)
                    pool.wait_ge(S["scaled"], prepared(L, i, ahead, 3))
                    nc.gpsimd.tensor_tensor(X, X, lnmb[:, :].unsqueeze(1).to_broadcast([P, KT, C]),
                                            ALU.add).then_inc(S["normed"], 1)
                    pool.wait_ge(S["normed"], done)
                pool.wait_ge(S["values_hi"], done)
                last = nc.gpsimd.tensor_tensor(Xlo[:, par, 0:KT, :], X, Xhi[:, par, 0:KT, :], ALU.subtract)
                if L.lat:
                    nc.gpsimd.tensor_tensor(Xlo[:NQ, par, KT, :],
                                            xq[:NQ, bass.ds(bq, 1), :].rearrange("p a c -> p (a c)"),
                                            Xhi[:NQ, par, KT, :], ALU.subtract)
                    last = nc.gpsimd.tensor_tensor(XTlo[:, par, LATC], xqT[:, bass.ds(bq * NQ, NQ)],
                                                   XThi[:, par, LATC], ALU.subtract)
                last.then_inc(S["values_done"], 1)

            def power(n):
                pool.wait_ge(S["var_ready"], n)
                nc.gpsimd.tensor_tensor(small[:NQ, 2, :], small[:NQ, 1, :], minus_half[:NQ, :],
                                        ALU.pow).then_inc(S["rstd_ready"], 1)

            pool.wait_ge(S["zeros_ready"], 1)
            power(1)
            power(2)
            pool.wait_ge(S["params_in"], 16 * PARAMS)
            for L in (L0, L1):
                if L is L1:
                    power(3)
                    power(4)
                if L.lat:
                    pool.wait_ge(S["glue_T_done"], GLUE)
                prepare(L, 0, 0, 0)
                with pool.Fori(0, LOOPS) as i:
                    prepare(L, i, 1, 2 * i + 1)
                    prepare(L, i, 2, 2 * i + 2)

            power(5)
            power(6)
            with pool.Fori(0, E // 2) as i:
                for J in range(CHUNKS + 2):
                    for f in range(FT):
                        if J < CHUNKS:
                            u = J * FT + f
                            pool.wait_ge(S["ahi_ready"], i * UNITS + u + 1)
                            nc.gpsimd.tensor_tensor(alo[:, J % 2, f, :], actf[:, u % 2, :], ahi[:, J % 2, f, :],
                                                    ALU.subtract).then_inc(S["alo_ready"], 1)
                        if J >= 2 and f == 2:
                            d = J % 2
                            pool.wait_ge(S["ms_ready"], i * CHUNKS + J - 1)
                            nc.gpsimd.tensor_tensor(coef[:NQ, d, 1, :], coef[:NQ, d, 0, :], minus_half[:NQ, 0:GROUP],
                                                    ALU.pow).then_inc(S["coef_ready"], 1)
            power(7)

        @block.tensor
        def _(pe):
            mm, tr = nc.tensor.matmul, nc.tensor.transpose
            pe.sem_inc(S["v_ready"], 1)
            pe.sem_inc(S["down_ready"], 2)

            pe.wait_ge(S["ident_ready"], 2)
            pe.wait_ge(S["weights_in"], 16 * WEIGHTS)
            for n, group in enumerate(FOLD):
                if n >= 4:
                    pe.wait_ge(S["fold_done"], n - 3)
                needs, _, _, members = group
                pe.wait_ge(S["fold_done"], needs)
                for s, (l, r) in enumerate(members):
                    o = score[:, n % 4, s * P:(s + 1) * P]
                    last = tr(o, l, ident[:, :]) if r is None else mm(o, l, r, start=True, stop=True)
                last.then_inc(S["fold_ready"], 1)
            for s, m in enumerate((0, 3, 4)):
                tr(side[:, s * P:(s + 1) * P], Wsm[:, m, :], ident[:, :])
            tr(side[:, 3 * P:3 * P + E], Wsm[0:E, 5, :], ident[0:E, 0:E]).then_inc(S["small_ready"], 1)
            pe.wait_ge(S["small_done"], 1)
            mm(side[:, 0:P], Wsm[:, 1, :], WsmT[:, 0, :], start=True, stop=True).then_inc(S["small_ready"], 1)
            pe.wait_ge(S["small_done"], 2)
            mm(side[:, 0:P], Wf[:, 0, :], Wsm[:, 2, :], start=True, stop=True).then_inc(S["small_ready"], 1)
            pe.wait_ge(S["small_done"], 3)

            def glue_transposes(n):
                for k in range(GLUE):
                    pe.wait_ge(S["xq_ready"], n + 1)
                    for s in range(GROUP):
                        b = k * GROUP + s
                        last = tr(score[:, k, s * NQ:(s + 1) * NQ], xq[:NQ, b, :], ident[:NQ, :NQ])
                    last.then_inc(S["glue_T_ready"], 1)

            pe.wait_ge(S["fold_done"], FOLDS)
            pe.wait_ge(S["null_ready"], 1)
            glue_transposes(0)
            pe.wait_ge(S["glue_T_done"], GLUE)

            def attention(L):
                A0 = 0 if L.lat else L0.heads

                def piece(i, idx, kind, par, k, bq):
                    pe.wait_ge(S["piece_done"], idx)
                    if kind == "Q":
                        for s in range(GROUP):
                            last = mm(side[:, s * NQ:(s + 1) * NQ], Amat[:, A0 + k * GROUP + s, :],
                                      xqT[:, bass.ds(bq * NQ, NQ)] if i is not None else xqT[:, 0:NQ],
                                      start=True, stop=True)
                    elif kind == "X":
                        for s in range(GROUP):
                            last = tr(side[:, s * P:(s + 1) * P], raw[:, par, k * GROUP + s, :], ident[:, :])
                    elif kind == "Z":
                        last = tr(side[:, 0:P], Zs[:, k, :], ident[:, :])
                    else:
                        for h in range(L.heads):
                            last = mm(side[:NQ, 0:C], ZT[:, par, h * NQ:(h + 1) * NQ], Mmat[:, A0 + h, :],
                                      start=(h == 0), stop=(h == L.heads - 1))
                    last.then_inc(S["piece_ready"], 1)

                for m, (kind, par, k) in enumerate(L.prologue):
                    if kind == "X":
                        if L.lat:
                            pe.wait_ge(S["normed"], prepared(L, 0, 0))
                        else:
                            pe.wait_ge(S["ctx_in0"], loaded(L, 0, 0))
                    piece(None, every.prologue(L, m), kind, par, k, 0)

                def scores(i, n, c):
                    bp, t = n // L.T, n % L.T
                    if t == 0 and c == 0:
                        m = operands_complete(L, 1) if bp else 0
                        pe.wait_ge(S["piece_done"], every.at(L, i, m))
                        pe.wait_ge(S["values_done"], prepared(L, i, bp))
                    if c % 2 == 0:
                        pe.wait_ge(S["score_copied"], copied_c.at(L, i, n - 1, c // 2 + 1))
                    qh, ql = (w[:, bp, t * P:(t + 1) * P] for w in (QThi, QTlo))
                    parts = [(slice(0, CH), slice(c * CH, (c + 1) * CH))]
                    if L.lat and c == 3:
                        parts.append((slice(CH, CH + NQ), LATC))
                    for o, s in parts:
                        out = score[:, c, o]
                        mm(out, qh, XThi[:, bp, s], start=True, stop=False)
                        mm(out, qh, XTlo[:, bp, s], start=False, stop=False)
                        last = mm(out, ql, XThi[:, bp, s], start=False, stop=True)
                    if c % 2:
                        last.then_inc(S["score_ready"], 1)

                def turn_group(i, n, k):
                    pe.wait_ge(S["exp_done"], exp_c.at(L, i, n))
                    pe.wait_ge(S["pt_lo"], ptlo_c.at(L, i, n, k - 1))
                    for s in range(min(GROUP, L.KT - k * GROUP)):
                        kt = k * GROUP + s
                        last = tr(turn[:, (n * L.groups + k) % 2, s * P:(s + 1) * P],
                                  prob[:, (n - 1) % 2, kt * P:(kt + 1) * P], ident[:, :])
                    last.then_inc(S["turned"], 1)

                def values(i, n, kts):
                    q, vp = n % 2, (n - 2) // L.T % 2
                    if kts[0] == 0:
                        pe.wait_ge(S["z_scaled"], z_c.at(L, i, n))
                        pe.wait_ge(S["pt_lo"], ptlo_c.at(L, i, n))
                    for kt in kts:
                        ph, pl = (w[:, q, kt * P:(kt + 1) * P] for w in (PThi, PTlo))
                        mm(vbank[:, 0:C], ph, Xhi[:, vp, kt, :], start=(kt == 0), stop=False)
                        mm(vbank[:, 0:C], ph, Xlo[:, vp, kt, :], start=False, stop=False)
                        last = mm(vbank[:, 0:C], pl, Xhi[:, vp, kt, :], start=False, stop=(kt == L.KT - 1))
                    if kts[-1] == L.KT - 1:
                        last.then_inc(S["v_ready"], 1)

                def step(i, n, m):
                    cuts = [range(0, 4), range(4, 9), range(9, L.KT)]
                    early = L.early
                    for c in range(4):
                        if n < L.N:
                            scores(i, n, c)
                        if n <= L.N and c % 2:
                            turn_group(i, n, c // 2)
                        if c == 1:
                            pe.wait_ge(S["z_scaled"], z_c.at(L, i, n))
                            piece(i, every.at(L, i, m), "Z", None, (n - 3) % 2, None)
                    if n <= L.N + 1:
                        values(i, n, cuts[0])
                    if n <= L.N:
                        for k in range(2, early):
                            turn_group(i, n, k)
                    for kind, par, k in L.sched[n][1:]:
                        m += 1
                        if kind == "X":
                            if L.lat:
                                pe.wait_ge(S["normed"], prepared(L, i, 2 - par))
                            else:
                                pe.wait_ge(S[f"ctx_in{par}"], loaded(L, i, 2 - par))
                        piece(i, every.at(L, i, m), kind, par, k, 2 * i + (2 - par) if kind == "Q" else None)
                    if n <= L.N + 1:
                        values(i, n, cuts[1])
                    if n <= L.N:
                        for k in range(early, L.groups):
                            turn_group(i, n, k)
                    if n <= L.N + 1:
                        values(i, n, cuts[2])
                    return m + 1

                with pe.Fori(0, LOOPS) as i:
                    m = 0
                    for n in range(L.N):
                        m = step(i, n, m)
                for n in range(L.N, L.N + 3):
                    m = step(LOOPS - 1, n, m)

            attention(L0)

            glue_transposes(1)
            pe.wait_ge(S["glue_T_done"], 2 * GLUE)

            def token_matmul(weights):
                for k in range(GLUE):
                    for s in range(GROUP):
                        b = k * GROUP + s
                        last = mm(score[:NQ, k, s * P:(s + 1) * P], xqT[:, b * NQ:(b + 1) * NQ], weights,
                                  start=True, stop=True)
                    last.then_inc(S["token_mm"], 1)

            token_matmul(Wf[:, 1, :])
            glue_transposes(2)
            pe.wait_ge(S["glue_T_done"], 3 * GLUE)
            attention(L1)

            glue_transposes(3)
            pe.wait_ge(S["glue_T_done"], 4 * GLUE)
            token_matmul(WsmT[:, 1, :])
            glue_transposes(4)
            pe.wait_ge(S["glue_T_done"], 5 * GLUE)
            for b in range(B):
                last = mm(vbank[:NQ, b * E:(b + 1) * E], xqT[:, b * NQ:(b + 1) * NQ], WsmT[:, 3, 0:E],
                          start=True, stop=True)
            last.then_inc(S["logits_ready"], 1)

            def turn_weights(ep, k, value, arrived):
                pe.wait_ge(S[f"moe_in{ep}"], arrived)
                pe.wait_ge(S["w_lo"], value)
                for s in range(FT):
                    last = tr(side[:, s * P:(s + 1) * P], wraw[:, (ep * 3 + k) * FT + s, :], ident[:, :])
                last.then_inc(S["w_turned"], 1)

            for k in range(3):
                turn_weights(0, k, k, 48)
            pe.wait_ge(S["h_split"], 1)
            with pe.Fori(0, E // 2) as i:
                for J in range(CHUNKS + 1):
                    for f in range(FT):
                        if J < CHUNKS:
                            ep, j, u = J // 4, J % 4, J * FT + f
                            if u % (4 * FT) == 0:
                                pe.wait_ge(S["w_lo"], i * 6 + 3 * ep + 3)
                            pe.wait_ge(S["act_ready"], i * UNITS + u + 1)
                            cols = slice(j * 4 * NQ, (j + 1) * 4 * NQ)
                            for w in range(2):
                                out = score[:, (u % 2) * 2 + w, 0:4 * NQ]
                                wh, wl = (v[:, ep, w, f * P:(f + 1) * P] for v in (wThi, wTlo))
                                mm(out, wh, hThi[:, cols], start=True, stop=False)
                                mm(out, wh, hTlo[:, cols], start=False, stop=False)
                                last = mm(out, wl, hThi[:, cols], start=False, stop=True)
                            last.then_inc(S["gu_ready"], 1)
                        if J >= 1:
                            D, s = J - 1, f
                            ep = D // 4
                            if s == 0:
                                pe.wait_ge(S["alo_ready"], i * UNITS + D * FT + FT + 1)
                                pe.wait_ge(S["down_copied"], i * CHUNKS + D + 1)
                            toks = slice(s * NQ, (s + 1) * NQ)
                            out = turn[:NQ, D % 2, s * P:(s + 1) * P]
                            for g in range(FT):
                                dh, dl = (v[:, ep, 2, g * P:(g + 1) * P] for v in (wThi, wTlo))
                                ah, al = (v[:, D % 2, g, toks] for v in (ahi, alo))
                                mm(out, ah, dh, start=(g == 0), stop=False)
                                mm(out, ah, dl, start=False, stop=False)
                                last = mm(out, al, dh, start=False, stop=(g == FT - 1))
                            if s == GROUP - 1:
                                last.then_inc(S["down_ready"], 1)
                    if J < CHUNKS and J % 4 < 3:
                        ep, k = J // 4, J % 4
                        turn_weights(1 - ep, k, i * 6 + 3 * (ep + 1) + k, (i + 1 + ep) * 48)
            glue_transposes(5)
            pe.wait_ge(S["glue_T_done"], 6 * GLUE)
            token_matmul(WsmT[:, 2, :])

        @block.scalar
        def _(act):
            fn = nc.scalar.activation
            act.sem_inc(S["exp_done"], 1)
            act.sem_inc(S["z_scaled"], 1)
            act.sem_inc(S["down_copied"], 2)
            act.wait_ge(S["null_ready"], 1)
            act.wait_ge(S["params_in"], 16 * PARAMS)
            fn(gt[:, :], gin[:, :], ACT.Tanh).then_inc(S["gates_tanh"], 1)
            act.wait_ge(S["gates_tanh"], 1)
            for n, group in enumerate(FOLD):
                act.wait_ge(S["fold_ready"], n + 1)
                _, dst, scale, _ = group
                src = score[:, n % 4, :].rearrange("p (s c) -> p s c", c=P)
                fn(dst, src, ACT.Copy, scale=scale).then_inc(S["fold_done"], 1)
            act.wait_ge(S["small_ready"], 1)
            fn(WsmT[:, 0:3, :], side[:, 0:3 * P].rearrange("p (s c) -> p s c", c=P), ACT.Copy)
            fn(WsmT[:, 3, 0:E], side[:, 3 * P:3 * P + E], ACT.Copy).then_inc(S["small_done"], 1)
            for s in range(2):
                act.wait_ge(S["small_ready"], 2 + s)
                fn(Wf[:, s, :], side[:, 0:P], ACT.Copy).then_inc(S["small_done"], 1)

            def glue_copies(n):
                for k in range(GLUE):
                    act.wait_ge(S["glue_T_ready"], n * GLUE + k + 1)
                    fn(xqT[:, qcols(k)], score[:, k, 0:GROUP * NQ], ACT.Copy).then_inc(S["glue_T_done"], 1)

            glue_copies(0)
            act.wait_ge(S["glue_T_done"], GLUE)

            def attention(L):
                def split_hi(kind, par, k, value):
                    act.wait_ge(S["piece_ready"], value)
                    if kind == "Q":
                        fn(QThi[:, par, qcols(k)], side[:, 0:GROUP * NQ], ACT.Copy).then_inc(S["piece_hi"], 1)
                    else:
                        cols = slice(k * GROUP * P, (k + 1) * GROUP * P)
                        fn(XThi[:, par, cols], side[:, :], ACT.Copy).then_inc(S["piece_hi"], 1)

                def values_hi(i, ahead, bq):
                    par = ahead % 2
                    if L.lat:
                        act.wait_ge(S["normed"], prepared(L, i, ahead))
                        fn(Xhi[:NQ, par, KT, :], xq[:NQ, bass.ds(bq, 1), :].rearrange("p a c -> p (a c)"), ACT.Copy)
                        fn(XThi[:, par, LATC], xqT[:, bass.ds(bq * NQ, NQ)], ACT.Copy)
                    else:
                        act.wait_ge(S[f"ctx_in{par}"], loaded(L, i, ahead))
                    fn(Xhi[:, par, 0:KT, :], raw[:, par, :, :], ACT.Copy).then_inc(S["values_hi"], 1)

                act.wait_ge(S["zeros_ready"], 1)
                for m, (kind, par, k) in enumerate(L.prologue):
                    if m == L.qgroups:
                        values_hi(0, 0, 0)
                    split_hi(kind, par, k, every.prologue(L, m) + 1)

                def step(i, n, m):
                    def pt_hi(groups):
                        for k in groups:
                            act.wait_ge(S["turned"], turned_c.at(L, i, n, k + 1))
                            if k == 0:
                                act.wait_ge(S["v_ready"], v_c.at(L, i, n))
                            w = min(GROUP, L.KT - k * GROUP) * P
                            fn(PThi[:, (n - 1) % 2, k * GROUP * P:k * GROUP * P + w],
                               turn[:, (n * L.groups + k) % 2, 0:w], ACT.Copy).then_inc(S["pt_hi"], 1)

                    if n <= L.N:
                        pt_hi(range(L.early))
                    for kind, par, k in L.sched[n]:
                        if kind in "QX":
                            split_hi(kind, par, k, every.at(L, i, m) + 1)
                        m += 1
                    if n < L.N:
                        p = n % 2
                        act.wait_ge(S["negm_ready"], negm_c.at(L, i, n, 1))
                        for s, cols in enumerate((slice(0, NK), LATC)[:L.sums]):
                            last = fn(prob[:, p, cols], prob[:, p, cols], ACT.Exp, bias=negm[:, p:p + 1],
                                      accum_out=lsum[:, p, s:s + 1])
                        last.then_inc(S["exp_done"], 1)
                    if n <= L.N:
                        pt_hi(range(L.early, L.groups))
                    if n <= L.N + 1:
                        act.wait_ge(S["v_ready"], v_c.at(L, i, n, 1))
                        act.wait_ge(S["rinv_ready"], rinv_c.at(L, i, n))
                        fn(Zs[:, n % 2, :], vbank[:, 0:C], ACT.Copy, scale=rinv[:, n % 2:n % 2 + 1]).then_inc(S["z_scaled"], 1)
                    if n < L.N and n % L.T == L.values_at:
                        ahead = n // L.T + 1
                        values_hi(i, ahead, 2 * i + ahead)
                    return m

                with act.Fori(0, LOOPS) as i:
                    m = 0
                    for n in range(L.N):
                        m = step(i, n, m)
                for n in range(L.N, L.N + 3):
                    m = step(LOOPS - 1, n, m)

            attention(L0)
            glue_copies(1)
            for k in range(GLUE):
                act.wait_ge(S["ffn_biased"], k + 1)
                fn(tmp[:NQ, k * GROUP:(k + 1) * GROUP, :], tmp[:NQ, k * GROUP:(k + 1) * GROUP, :],
                   ACT.Tanh).then_inc(S["ffn_tanh"], 1)
            glue_copies(2)
            attention(L1)
            glue_copies(3)
            glue_copies(4)
            act.wait_ge(S["glue_T_done"], 5 * GLUE)
            fn(hThi[:, 0:B * NQ], xqT[:, 0:B * NQ], ACT.Copy).then_inc(S["h_hi"], 1)
            act.wait_ge(S["route_ready"], 1)
            fn(route[:NQ, 5, :], route[:NQ, 4, :], ACT.Exp).then_inc(S["route_exp"], 1)

            def weights_hi(ep, k, value):
                act.wait_ge(S["w_turned"], value)
                fn(wThi[:, ep, k, :], side[:, :], ACT.Copy, scale=WSCALE).then_inc(S["w_hi"], 1)

            for k in range(3):
                weights_hi(0, k, k + 1)
            with act.Fori(0, E // 2) as i:
                for J in range(CHUNKS + 2):
                    for f in range(FT):
                        if J < CHUNKS:
                            u = J * FT + f
                            act.wait_ge(S["gu_ready"], i * UNITS + u + 1)
                            fn(sil[:, u % 2, :], score[:, (u % 2) * 2, 0:4 * NQ], ACT.Silu,
                               scale=1.0 / WSCALE).then_inc(S["sil_ready"], 1)
                        if J >= 2 and f < 2:
                            D = J - 2
                            if f == 0:
                                act.wait_ge(S["down_ready"], i * CHUNKS + D + 3)
                                act.wait_ge(S["acc_ready"], i * CHUNKS + D + 1)
                                fn(dsb[:NQ, D % 2, :, :], turn[:NQ, D % 2, :].rearrange("p (s c) -> p s c", c=C),
                                   ACT.Copy).then_inc(S["down_copied"], 1)
                                act.wait_ge(S["down_copied"], i * CHUNKS + D + 3)
                            for s in (2 * f, 2 * f + 1):
                                last = fn(sqs[:NQ, D % 2, s, :], dsb[:NQ, D % 2, s, :], ACT.Square,
                                          scale=1.0 / WSCALE ** 2, accum_out=ssq[:NQ, D % 2, s:s + 1])
                            if f == 1:
                                last.then_inc(S["sq_ready"], 1)
                    if J < CHUNKS and J % 4 < 3:
                        ep, k = J // 4, J % 4
                        weights_hi(1 - ep, k, i * 6 + 3 * (ep + 1) + k + 1)
            glue_copies(5)

        @block.vector
        def _(dve):
            v = nc.vector
            chain, norms = [0], [0]

            def link(ins):
                chain[0] += 1
                ins.then_inc(S["dve_chain"], 1)
                dve.wait_ge(S["dve_chain"], chain[0])

            dve.sem_inc(S["pt_lo"], 2)
            dve.sem_inc(S["score_copied"], 2)
            dve.sem_inc(S["rinv_ready"], 1)
            dve.sem_inc(S["act_ready"], 2)
            dve.sem_inc(S["acc_ready"], 2)

            def wide(stat):
                return stat.unsqueeze(2).to_broadcast([NQ, B, C])

            def over(vec):
                return vec.unsqueeze(1).to_broadcast([NQ, B, C])

            def norm(src, dst, eps, mean=True, ready=None):
                s0, s1, s2 = (small[:NQ, k, :] for k in range(3))
                if mean:
                    link(v.reduce_sum(s0, src, AX.X))
                    link(v.tensor_scalar(s1, s0, 1.0 / C, None, ALU.mult))
                    link(v.tensor_tensor(dst, src, wide(s1), ALU.subtract))
                    src = dst
                link(v.tensor_tensor(tmp[:NQ, :, :], src, src, ALU.mult))
                link(v.reduce_sum(s0, tmp[:NQ, :, :], AX.X))
                v.tensor_scalar(s1, s0, 1.0 / C, eps, ALU.mult, ALU.add).then_inc(S["var_ready"], 1)
                norms[0] += 1
                dve.wait_ge(S["rstd_ready"], norms[0])
                last = v.tensor_tensor(dst, src, wide(s2), ALU.mult)
                link(last) if ready is None else last.then_inc(ready, 1)

            v.memset(prob[:, 1, 0:NK], 0.0)
            v.memset(Xhi[:, 1, 0:KT, :], 0.0)
            v.memset(Xlo[:, 1, 0:KT, :], 0.0)
            v.memset(PThi[:, 0, :], 0.0)
            v.memset(PTlo[:, 0, :], 0.0)
            v.memset(ZT[:, 1, :], 0.0)
            v.memset(Zs[:, :, :], 0.0)
            v.memset(x[:, 0, :], 0.0)
            v.memset(rinv[:, :], 1.0)
            v.memset(lsum[:, :, :], 1.0).then_inc(S["null_ready"], 1)
            xv, xn = x[:NQ, 1:, :], xq[:NQ, 0:B, :]
            dve.wait_ge(S["zeros_ready"], 1)
            dve.wait_ge(S["x_in"], 16)
            norm(xv, xn, LN_EPS)
            norm(xn, xn, LN_EPS)
            dve.wait_ge(S["params_in"], 16 * PARAMS)
            link(v.tensor_tensor(xn, xn, over(lnlw[:NQ, :]), ALU.mult))
            v.tensor_tensor(xn, xn, over(lnlb[:NQ, :]), ALU.add).then_inc(S["xq_ready"], 1)
            dve.wait_ge(S["gates_tanh"], 1)
            link(v.tensor_scalar(obias[:, :], obias[:, :], gt[:, 1:2], None, ALU.mult))

            def attention(L):
                def row_stats(i, ahead, quarter):
                    par, each = ahead % 2, KT // 4
                    if quarter == 0:
                        dve.wait_ge(S[f"ctx_in{par}"], loaded(L, i, ahead))
                    for t in range(quarter * each, (quarter + 1) * each):
                        last = v.bn_stats(stat6[:, t, :], raw[:, par, t, :])
                    if quarter == 3:
                        last.then_inc(S["stat_step"], 1)

                def stats(i, ahead):
                    done = prepared(L, i, ahead)
                    dve.wait_ge(S["stat_step"], prepared(L, i, ahead, 2) - 1)
                    dve.sem_inc(S["waited"], 1)
                    for t in range(KT):
                        last = v.bn_aggr(mv[:, t, :], stat6[:, t, :])
                    last.then_inc(S["stat_step"], 1)
                    dve.wait_ge(S["stat_step"], prepared(L, i, ahead, 2))
                    dve.wait_ge(S["normed"], done - 1)
                    v.tensor_scalar(nmean_k[:, :], mv[:, :, 0], -1.0, None, ALU.mult)
                    v.tensor_scalar(var_k[:, :], mv[:, :, 1], LN_EPS, None, ALU.add).then_inc(S["stats_ready"], 1)

                def split_lo(kind, par, k, value):
                    dve.wait_ge(S["piece_hi"], value)
                    if kind == "Q":
                        v.tensor_tensor(QTlo[:, par, qcols(k)], side[:, 0:GROUP * NQ], QThi[:, par, qcols(k)],
                                        ALU.subtract).then_inc(S["piece_done"], 1)
                    else:
                        cols = slice(k * GROUP * P, (k + 1) * GROUP * P)
                        v.tensor_tensor(XTlo[:, par, cols], side[:, :], XThi[:, par, cols],
                                        ALU.subtract).then_inc(S["piece_done"], 1)

                if L.lat:
                    for quarter in range(4):
                        row_stats(0, 0, quarter)
                    stats(0, 0)
                for m, (kind, par, k) in enumerate(L.prologue):
                    split_lo(kind, par, k, split.prologue(L, m) + 1)
                def copy_max(n, banks, cols, part):
                    out = prob[:, n % 2, cols]
                    if len(banks.shape) == 3:
                        out = out.rearrange("p (b c) -> p b c", b=2)
                    return v.tensor_scalar(out, banks, 1.0, None, ALU.mult, ALU.max, accum_out=mx[:, n % 2, part:part + 1])

                def pt_lo(i, n, k):
                    dve.wait_ge(S["pt_hi"], pthi_c.at(L, i, n, k + 1))
                    w = min(GROUP, L.KT - k * GROUP) * P
                    out = slice(k * GROUP * P, k * GROUP * P + w)
                    v.tensor_tensor(PTlo[:, (n - 1) % 2, out], turn[:, (n * L.groups + k) % 2, 0:w],
                                    PThi[:, (n - 1) % 2, out], ALU.subtract).then_inc(S["pt_lo"], 1)

                def step(i, n, m):
                    p, q = n % 2, (n - 1) % 2
                    if L.lat and n < L.N and n % L.T < 2:
                        row_stats(i, n // L.T + 1, 2 * (n % L.T))
                    if L.lat and n < L.N and n % L.T == 2:
                        stats(i, n // L.T + 1)
                    if n < L.N:
                        dve.wait_ge(S["score_ready"], score_c.at(L, i, n, 1))
                        copy_max(n, score[:, 0:2, 0:CH], slice(0, 2 * CH), 0).then_inc(S["score_copied"], 1)
                    _, par, k = L.sched[n][0]
                    dve.wait_ge(S["piece_ready"], every.at(L, i, m) + 1)
                    v.tensor_copy(ZT[:, par, k * P:(k + 1) * P], side[:, 0:P]).then_inc(S["piece_done"], 1)
                    if n <= L.N:
                        pt_lo(i, n, 0)
                    if n < L.N:
                        dve.wait_ge(S["score_ready"], score_c.at(L, i, n, 2))
                        last = copy_max(n, score[:, 2:4, 0:CH], slice(2 * CH, NK), 1)
                        if L.lat:
                            last = copy_max(n, score[:, 3, CH:CH + NQ], LATC, 2)
                        last.then_inc(S["score_copied"], 1)
                        dve.wait_ge(S["score_copied"], copied_c.at(L, i, n, 2))
                        v.reduce_max(negm[:, p:p + 1], mx[:, p, 0:L.maxes], AX.X, negate=True).then_inc(S["negm_ready"], 1)
                    if n <= L.N:
                        for k in range(1, L.early):
                            pt_lo(i, n, k)
                    for kind, par, k in L.sched[n][1:]:
                        m += 1
                        if kind in "QX":
                            split_lo(kind, par, k, split.at(L, i, m) + 1)
                        else:
                            dve.wait_ge(S["piece_ready"], every.at(L, i, m) + 1)
                            xb = x[:NQ, bass.ds(2 * i + k, 1), :].rearrange("p a c -> p (a c)")
                            v.tensor_tensor(xb, side[:NQ, 0:C], xb, ALU.add).then_inc(S["piece_done"], 1)
                    if n <= L.N:
                        dve.wait_ge(S["z_scaled"], z_c.at(L, i, n))
                        dve.wait_ge(S["exp_done"], exp_c.at(L, i, n))
                        src = lsum[:, q, 0:1]
                        if L.sums > 1:
                            v.tensor_tensor(lall[:, q:q + 1], lsum[:, q, 0:1], lsum[:, q, 1:2], ALU.add).then_inc(S["sum_ready"], 1)
                            dve.wait_ge(S["sum_ready"], i * L.N + (n + 1))
                            src = lall[:, q:q + 1]
                        v.reciprocal(rinv[:, q:q + 1], src).then_inc(S["rinv_ready"], 1)
                        for k in range(L.early, L.groups):
                            pt_lo(i, n, k)
                    if L.lat and n < L.N and n % L.T < 2:
                        row_stats(i, n // L.T + 1, 2 * (n % L.T) + 1)
                    return m + 1

                with dve.Fori(0, LOOPS) as i:
                    m = 0
                    for n in range(L.N):
                        m = step(i, n, m)
                for n in range(L.N, L.N + 3):
                    m = step(LOOPS - 1, n, m)

            attention(L0)
            dve.wait_ge(S["piece_done"], every.at(L0, LOOPS - 1, len(L0.flat + L0.tail)))
            dve.wait_ge(S["values_done"], prepared(L0, LOOPS - 1, 2))
            norm(xv, xn, LN_EPS, ready=S["xq_ready"])
            for k in range(GLUE):
                part = tmp[:NQ, k * GROUP:(k + 1) * GROUP, :]
                dve.wait_ge(S["token_mm"], k + 1)
                ps = score[:NQ, k, :].rearrange("p (s c) -> p s c", c=C)
                v.tensor_tensor(part, ps, fbias[:NQ, :].unsqueeze(1).to_broadcast([NQ, GROUP, C]),
                                ALU.add).then_inc(S["ffn_biased"], 1)
            for k in range(GLUE):
                part = tmp[:NQ, k * GROUP:(k + 1) * GROUP, :]
                xk = xv[:, k * GROUP:(k + 1) * GROUP, :]
                dve.wait_ge(S["ffn_tanh"], k + 1)
                link(v.scalar_tensor_tensor(out=xk, in0=part, scalar=gt[:NQ, 2:3], in1=xk, op0=ALU.mult, op1=ALU.add))
            norm(xv, xn, LN_EPS, ready=S["xq_ready"])
            link(v.tensor_tensor(xv, xv, over(obias[:NQ, :]), ALU.add))
            attention(L1)
            dve.wait_ge(S["piece_done"], every.at(L1, LOOPS - 1, len(L1.flat + L1.tail)))
            norm(xv, xn, LN_EPS, ready=S["xq_ready"])
            for k in range(GLUE):
                dve.wait_ge(S["token_mm"], GLUE + k + 1)
                link(v.tensor_copy(xq[:NQ, k * GROUP:(k + 1) * GROUP, :],
                                   score[:NQ, k, :].rearrange("p (s c) -> p s c", c=C)))
            norm(xn, xn, RMS_EPS, mean=False)
            v.tensor_tensor(xn, xn, over(innw[:NQ, :]), ALU.mult).then_inc(S["xq_ready"], 1)
            dve.wait_ge(S["h_hi"], 1)
            v.tensor_tensor(hTlo[:, 0:B * NQ], xqT[:, 0:B * NQ], hThi[:, 0:B * NQ], ALU.subtract).then_inc(S["h_split"], 1)

            R = [route[:NQ, k, :].rearrange("p (b e) -> p b e", e=E) for k in range(8)]
            st = [small[:NQ, k, :] for k in range(8)]

            def each(s):
                return s.unsqueeze(2).to_broadcast([NQ, B, E])

            io = iota8[:NQ, :].unsqueeze(1).to_broadcast([NQ, B, E])
            dve.wait_ge(S["logits_ready"], 1)
            link(v.tensor_copy(R[0], vbank[:NQ, 0:B * E].rearrange("p (b e) -> p b e", e=E)))
            link(v.tensor_tensor(R[1], R[0], ebias[:NQ, :].unsqueeze(1).to_broadcast([NQ, B, E]), ALU.add))
            for pick in (2, 3):
                link(v.reduce_max(st[0], R[1], AX.X))
                link(v.tensor_tensor(R[6], R[1], each(st[0]), ALU.is_equal))
                link(v.tensor_tensor(R[7], R[6], io, ALU.mult))
                link(v.tensor_reduce(st[1], R[7], AX.X, ALU.min))
                link(v.tensor_tensor(R[pick], io, each(st[1]), ALU.is_equal))
                link(v.scalar_tensor_tensor(out=R[1], in0=R[pick], scalar=-3.0e38, in1=R[1], op0=ALU.mult, op1=ALU.add))
            link(v.tensor_tensor(R[2], R[2], R[3], ALU.add))
            link(v.tensor_scalar(R[3], R[2], -1.0, 3.0e38, ALU.add, ALU.mult))
            link(v.tensor_tensor(R[3], R[3], R[0], ALU.add))
            link(v.reduce_max(st[0], R[3], AX.X))
            link(v.tensor_tensor(R[6], R[0], each(st[0]), ALU.subtract))
            link(v.tensor_tensor(R[6], R[6], R[2], ALU.mult))
            v.tensor_copy(R[4], R[6]).then_inc(S["route_ready"], 1)
            dve.wait_ge(S["route_exp"], 1)
            link(v.tensor_tensor(R[5], R[5], R[2], ALU.mult))
            link(v.reduce_sum(st[0], R[5], AX.X))
            link(v.reciprocal(st[1], st[0]))
            link(v.tensor_tensor(R[0], R[5], each(st[1]), ALU.mult))
            link(v.memset(tmp[:NQ, :, :], 0.0))

            def weights_lo(ep, k, value):
                dve.wait_ge(S["w_hi"], value)
                v.scalar_tensor_tensor(out=wTlo[:, ep, k, :], in0=side[:, :], scalar=WSCALE, in1=wThi[:, ep, k, :],
                                       op0=ALU.mult, op1=ALU.subtract).then_inc(S["w_lo"], 1)

            for k in range(3):
                weights_lo(0, k, k + 1)
            with dve.Fori(0, E // 2) as i:
                for J in range(CHUNKS + 3):
                    for f in range(FT):
                        if J < CHUNKS:
                            u = J * FT + f
                            dve.wait_ge(S["sil_ready"], i * UNITS + u + 1)
                            dve.wait_ge(S["alo_ready"], i * UNITS + max(u, 1))
                            v.tensor_tensor(actf[:, u % 2, :], score[:, (u % 2) * 2 + 1, 0:4 * NQ], sil[:, u % 2, :],
                                            ALU.mult).then_inc(S["act_ready"], 1)
                            dve.wait_ge(S["act_ready"], i * UNITS + u + 3)
                            if f == 0:
                                dve.wait_ge(S["down_ready"], i * CHUNKS + J + 1)
                            v.tensor_copy(ahi[:, J % 2, f, :], actf[:, u % 2, :]).then_inc(S["ahi_ready"], 1)
                        if J >= 3:
                            D, j = J - 3, (J - 3) % 4
                            e = 2 * i + D // 4
                            d = D % 2
                            base = i * (2 * CHUNKS) + 2 * D
                            if f == 0:
                                dve.wait_ge(S["coef_ready"], i * CHUNKS + D + 1)
                                gate = route[:NQ, 0, :].rearrange("p (b e) -> p b e", e=E)[:, j * 4:(j + 1) * 4, bass.ds(e, 1)]
                                v.scalar_tensor_tensor(out=coef[:NQ, d, 2, :].unsqueeze(2),
                                                       in0=coef[:NQ, d, 1, :].unsqueeze(2), scalar=1.0 / WSCALE ** 2,
                                                       in1=gate, op0=ALU.mult, op1=ALU.mult).then_inc(S["coef_step"], 1)
                                dve.wait_ge(S["coef_step"], base + 1)
                            last = v.scalar_tensor_tensor(
                                out=term[:NQ, d, f, :], in0=dsb[:NQ, d, f, :], scalar=coef[:NQ, d, 2, f:f + 1],
                                in1=enw[:NQ, bass.ds(e, 1), :].rearrange("p a c -> p (a c)"), op0=ALU.mult, op1=ALU.mult)
                            if f == 3:
                                last.then_inc(S["coef_step"], 1)
                                dve.wait_ge(S["coef_step"], base + 2)
                                v.tensor_tensor(tmp[:NQ, j * 4:(j + 1) * 4, :], tmp[:NQ, j * 4:(j + 1) * 4, :],
                                                term[:NQ, d, :, :], ALU.add).then_inc(S["acc_ready"], 1)
                        if 2 <= J < CHUNKS + 2 and f == 1:
                            dve.wait_ge(S["sq_ready"], i * CHUNKS + J - 1)
                            v.tensor_scalar(coef[:NQ, J % 2, 0, :], ssq[:NQ, J % 2, :], 1.0 / C, RMS_EPS, ALU.mult,
                                            ALU.add).then_inc(S["ms_ready"], 1)
                    if J < CHUNKS and J % 4 < 3:
                        ep, k = J // 4, J % 4
                        weights_lo(1 - ep, k, i * 6 + 3 * (ep + 1) + k + 1)
            dve.wait_ge(S["acc_ready"], E // 2 * CHUNKS + 2)
            link(v.tensor_copy(xn, tmp[:NQ, :, :]))
            norm(xn, xn, RMS_EPS, mean=False)
            v.tensor_tensor(xn, xn, over(outnw[:NQ, :]), ALU.mult).then_inc(S["xq_ready"], 1)
            for k in range(GLUE):
                dve.wait_ge(S["token_mm"], 2 * GLUE + k + 1)
                xk = xv[:, k * GROUP:(k + 1) * GROUP, :]
                last = v.scalar_tensor_tensor(out=xk, in0=score[:NQ, k, :].rearrange("p (s c) -> p s c", c=C),
                                              scalar=gt[:NQ, 3:4], in1=xk, op0=ALU.mult, op1=ALU.add)
            last.then_inc(S["x_final"], 1)


_INS = ['x', 'ctx_1024', 'g_xattn', 'g_ffn', 'L0_xattn_ln_m_w', 'L0_xattn_ln_m_b', 'L0_xattn_ln_l_w',
        'L0_xattn_ln_l_b', 'L0_xattn_Wq', 'L0_xattn_Wkv', 'L0_xattn_Wout', 'L0_ffn_weight', 'L0_ffn_aux_weight1',
        'L0_ffn_aux_weight2', 'L0_ffn_bias', 'L1_xattn_Wq', 'L1_xattn_Wk', 'L1_xattn_Wv', 'L1_xattn_Wo',
        'L1_xattn_bo', 'L1_ffn_W_in', 'L1_ffn_in_norm_w', 'L1_ffn_Wr', 'L1_ffn_expert_bias', 'L1_ffn_Wg',
        'L1_ffn_Wu', 'L1_ffn_Wd', 'L1_ffn_enorm_w', 'L1_ffn_out_norm_w', 'L1_ffn_W_out']
_OUTS = [((B, NQ, C), 'float32')]


def kernel(**inputs):
    import numpy as _np
    import concourse.bacc as _bacc
    from concourse import mybir as _mybir
    from concourse.bass_utils import run_bass_kernel_spmd as _run

    nc = _bacc.Bacc("TRN2", target_bir_lowering=False, num_devices=1)
    arrays, args = {}, {}
    for name in _INS:
        a = _np.ascontiguousarray(inputs[name])
        arrays[f"in_{name}_dram"] = a
        args[name] = nc.dram_tensor(f"in_{name}_dram", a.shape, _mybir.dt.from_np(a.dtype), kind="ExternalInput").ap()
    for i, (shape, dtype) in enumerate(_OUTS):
        dt = _mybir.dt.from_np(_np.dtype(dtype))
        args["out"] = nc.dram_tensor(f"out_{i}_dram", shape, dt, kind="ExternalOutput").ap()
    flamingo_kernel(nc, args)
    r = _run(nc, [arrays], core_ids=[0])
    return r.results[0]["out_0_dram"]
```

```python
from contextlib import ExitStack

import concourse.bass as bass
from concourse import mybir

F32 = mybir.dt.float32
F16 = mybir.dt.float16
ALU = mybir.AluOpType
ACT = mybir.ActivationFunctionType
AX = mybir.AxisListType

P = 128
B, NQ, C = 16, 100, 128
NK = 1444
KT = (NK + P - 1) // P
KLAST = NK - (KT - 1) * P
CH = NK // 4
DH = 64
LN_EPS = 1e-5
RMS_EPS = 1.1920928955078125e-07
E, FF = 8, 512
FT = FF // P
WSCALE = 256.0
GROUP = 4


class Layer:

    def __init__(self, index, heads, with_latents):
        self.index = index
        self.heads = heads
        self.lat = with_latents
        self.T = (heads * NQ + P - 1) // P
        self.N = 2 * self.T
        self.KT = KT + (1 if with_latents else 0)
        self.groups = (self.KT + GROUP - 1) // GROUP
        self.qgroups = heads // GROUP
        self.early = 3
        self.maxes = 3 if with_latents else 2
        self.sums = 2 if with_latents else 1
        self.values_at = 4 if with_latents else 2
        first_q, first_x = (1, 4) if with_latents else (4, 8)
        self.sched = [[] for _ in range(self.N + 3)]
        for n in range(self.N + 3):
            self.sched[n].append(("Z", 0 if 3 <= n < self.T + 3 else 1, (n - 3) % self.T))
            if n % self.T == 3 and n < self.N:
                self.sched[n].append(("O", 1 - n // self.T, n // self.T))
            if n < self.N:
                t, into = n % self.T, 1 - n // self.T
                if first_q <= t < first_q + self.qgroups:
                    self.sched[n].append(("Q", into, t - first_q))
                if first_x <= t < first_x + 3:
                    self.sched[n].append(("X", into, t - first_x))
        self.sched[self.N + 2].append(("O", 1, 2))
        queries, context = [("Q", 0, k) for k in range(self.qgroups)], [("X", 0, k) for k in range(3)]
        self.prologue = queries + context if with_latents else context + queries
        self.glue_at = None if with_latents else len(context)
        self.flat = [s for step in self.sched[:self.N] for s in step]
        self.tail = [s for step in self.sched[self.N:] for s in step]


L0 = Layer(0, 8, True)
L1 = Layer(1, 16, False)
LOOPS = B // 2


class Count:

    def __init__(self, per0, per1, extra=0, credit=0):
        self.per = (per0, per1)
        self.base = (credit, credit + per0 * (LOOPS * L0.N + extra))

    def at(self, layer, i, n, k=0):
        per = self.per[layer.index]
        return i * (per * layer.N) + (self.base[layer.index] + per * n + k)


def flamingo_kernel(nc, a):
    ctx = ExitStack()
    with ctx:
        def sb(name, shape, dt=F32):
            return ctx.enter_context(nc.sbuf_tensor(name, shape, dt))

        def sem(name):
            return ctx.enter_context(nc.semaphore(name))

        x = sb("x", [P, B + 1, C])
        xq = sb("xq", [P, B + 1, C])
        xqT = sb("xqT", [P, (B + 1) * NQ])
        tmp = sb("tmp", [P, B, C])
        raw = sb("raw", [P, 2, KT, C])
        Xhi = sb("Xhi", [P, 2, KT + 1, C], F16)
        Xlo = sb("Xlo", [P, 2, KT + 1, C], F16)
        KW = (KT + 1) * P
        XThi = sb("XThi", [P, 2, KW], F16)
        XTlo = sb("XTlo", [P, 2, KW], F16)
        QW = L1.T * P
        QThi = sb("QThi", [P, 2, QW], F16)
        QTlo = sb("QTlo", [P, 2, QW], F16)
        prob = sb("prob", [P, 2, KW])
        PThi = sb("PThi", [P, 2, KW], F16)
        PTlo = sb("PTlo", [P, 2, KW], F16)
        Zs = sb("Zs", [P, 2, C])
        ZT = sb("ZT", [P, 2, QW])
        Amat = sb("Amat", [P, L0.heads + L1.heads, C])
        Mmat = sb("Mmat", [P, L0.heads + L1.heads, C])
        ident = sb("ident", [P, P])
        mx = sb("mx", [P, 2, 4])
        negm = sb("negm", [P, 2])
        lsum = sb("lsum", [P, 2, 4])
        lall = sb("lall", [P, 2])
        rinv = sb("rinv", [P, 2])
        stat6 = sb("stat6", [P, B, 6])
        mvx = sb("mvx", [P, B, 2])
        mv = sb("mv", [P, KT, 2])
        rstd_k = sb("rstd_k", [P, KT])
        nmean_k = sb("nmean_k", [P, KT])
        lnmw = sb("lnmw", [P, C])
        lnmb = sb("lnmb", [P, C])
        lnlw = sb("lnlw", [P, C])
        lnlb = sb("lnlb", [P, C])
        fbias = sb("fbias", [P, C])
        obias = sb("obias", [P, C])
        innw = sb("innw", [P, C])
        outnw = sb("outnw", [P, C])
        enw = sb("enw", [P, E, C])
        ebias = sb("ebias", [P, E])
        gin = sb("gin", [P, 4])
        gt = sb("gt", [P, 4])
        small = sb("small", [P, 8, B])
        Wsm = sb("Wsm", [P, 6, C])
        WsmT = sb("WsmT", [P, 4, C])
        Wf = sb("Wf", [P, 2, C])
        route = sb("route", [P, 8, B * E])
        iota8 = sb("iota8", [P, E])
        var_k = sb("var_k", [P, KT])
        minus_half = sb("minus_half", [P, B])
        coef = sb("coef", [P, 2, 3, GROUP])
        ssq = sb("ssq", [P, 2, GROUP])
        hThi, hTlo = QThi[:, 0, :], QTlo[:, 0, :]
        wThi, wTlo = (w[:, :, 0:3 * FT * P].rearrange("p b (k f) -> p b k f", k=3) for w in (XThi, XTlo))
        ahi, alo = (w[:, :, 0:FT * 4 * NQ].rearrange("p b (f n) -> p b f n", f=FT) for w in (PThi, PTlo))
        sil, actf = prob[:, :, 0:4 * NQ], prob[:, :, 4 * NQ:8 * NQ]
        sqs, term, dsb = (ZT[:, :, s * 512:(s + 1) * 512].rearrange("p b (s c) -> p b s c", c=C) for s in range(3))
        LATC = slice(KT * P, KT * P + NQ)

        wraw = sb("wraw", [P, 48, C])
        wT = sb("wT", [P, 20, C])

        score = ctx.enter_context(nc.psum_tensor("score", [P, 4, 512], F32))
        turn = ctx.enter_context(nc.psum_tensor("turn", [P, 2, 512], F32))
        vbank = ctx.enter_context(nc.psum_tensor("vbank", [P, 512], F32))
        side = ctx.enter_context(nc.psum_tensor("side", [P, 512], F32))

        S = {n: sem(n) for n in """waited down_copied null_ready score_copied var_ready rstd_ready ms_ready coef_ready acc_ready act_ready ahi_ready alo_ready coef_step ctx_in0 ctx_in1 down_ready dve_chain
            exp_done ffn_biased ffn_tanh fold_done fold_ready gates_tanh glue_T_done
            glue_T_ready gu_ready h_hi h_split ident_ready logits_ready moe_in0
            moe_in1 negm_ready normed out_in params_in piece_done piece_hi piece_ready
            pt_hi pt_lo rinv_ready route_exp route_ready scaled score_ready sil_ready
            small_done small_ready sq_ready stat_step stats_ready sum_ready token_mm
            turned v_ready values_done values_hi w_hi w_lo w_turned weights_in x_final
            x_in first_weights_in norm_params_in pad_ready xq_ready z_scaled zeros_ready""".split()}

        score_c = Count(2, 2)
        copied_c = Count(2, 2, credit=2)
        negm_c = Count(1, 1)
        exp_c = Count(1, 1, credit=1)
        turned_c = Count(L0.groups, L1.groups, extra=1)
        pthi_c = Count(L0.groups, L1.groups, extra=1)
        ptlo_c = Count(L0.groups, L1.groups, extra=1, credit=2)
        rinv_c = Count(1, 1, extra=1, credit=1)
        v_c = Count(1, 1, extra=2, credit=1)
        z_c = Count(1, 1, extra=2, credit=1)

        class PieceCount:

            def __init__(self, kinds):
                def n(seq):
                    return sum(s[0] in kinds for s in seq)
                self.kinds = kinds
                self.loop = (n(L0.flat), n(L1.flat))
                self.pro = (n(L0.prologue), n(L1.prologue))
                self.start = (0, self.pro[0] + LOOPS * self.loop[0] + n(L0.tail))

            def prologue(self, layer, m):
                return self.start[layer.index] + sum(s[0] in self.kinds for s in layer.prologue[:m])

            def at(self, layer, i, m):
                done = sum(s[0] in self.kinds for s in (layer.flat + layer.tail)[:m])
                return i * self.loop[layer.index] + (self.start[layer.index] + self.pro[layer.index] + done)

        every = PieceCount("ZOQX")
        split = PieceCount("QX")

        def operands_complete(layer, par):
            last = [m for m, s in enumerate(layer.flat) if s[0] in "QX" and s[1] == par]
            return max(last) + 1

        PREPARED = B + 1

        def prepared(layer, i, ahead, per=1):
            return i * (2 * per) + (PREPARED * layer.index + ahead + 1) * per

        def loaded(layer, i, ahead):
            return i * 32 + ((LOOPS + 1) * layer.index + ahead // 2 + 1) * 32

        GLUE = B // GROUP
        CHUNKS, UNITS = 8, 8 * FT
        NORM_PARAMS, PARAMS = 6, 6
        FIRST_WEIGHTS, WEIGHTS = 3, 10

        def half(block, h):
            return block[(h % 2) * DH:(h % 2 + 1) * DH, :]

        def fold_groups():
            def turns(src, dst):
                return (0, wT[:, dst:dst + 4, :], 1.0, [(wraw[:, src + s, :], None) for s in range(4)])
            out = [turns(0, 0), turns(4, 4), turns(8, 8)]
            for L, lq, lk, lv, lo in ((L0, (wT, 0), (wT, 4), (wT, 8), (wraw, 12)),
                                      (L1, (wraw, 16), (wraw, 24), (wraw, 32), (wT, 12))):
                first = L0.heads * L.index
                if L is L1:
                    out += [turns(40, 12), turns(44, 16)]
                turned = len(out)
                for dst, l, r, scale in ((Amat, lq, lk, DH ** -0.5),
                                               (Mmat, lv, lo, gt[:, L.index:L.index + 1])):
                    for h0 in [g * 8 + par for g in range(L.heads // 8) for par in range(2)]:
                        out.append((turned, dst[:, first + h0:first + h0 + 7:2, :], scale,
                                    [(half(l[0][:, l[1] + h // 2, :], h), half(r[0][:, r[1] + h // 2, :], h))
                                     for h in range(h0, h0 + 8, 2)]))
            return out

        FOLD = fold_groups()
        FOLDS = len(FOLD)
        FIRST_FOLDS = 3 + 2 * L0.heads // GROUP

        def qcols(k):
            return slice(k * GROUP * NQ, (k + 1) * GROUP * NQ)

        block = ctx.enter_context(nc.Block())

        @block.sync
        def _(sp):
            def row(v):
                return v.rearrange("(a c) -> a c", a=1)

            def small_param(dst, src, done):
                sp.dma_start(dst, row(a[src]).to_broadcast([P, dst.shape[1]])).then_inc(S[done], 16)

            def load(src, par):
                full = src[0:(KT - 1) * P, :].rearrange("(t p) c -> p t c", p=P)
                sp.dma_start(raw[:, par, 0:KT - 1, :], full).then_inc(S[f"ctx_in{par}"], 16)
                sp.dma_start(raw[:KLAST, par, KT - 1, :], src[(KT - 1) * P:NK, :]).then_inc(S[f"ctx_in{par}"], 16)

            sp.dma_start(x[:NQ, 1:, :], a["x"].rearrange("b q c -> q b c")).then_inc(S["x_in"], 16)
            sp.wait_ge(S["pad_ready"], 1)
            load(a["ctx_1024"][0], 0)
            for at, n, src in ((0, 4, a["L0_xattn_Wq"].rearrange("c (k e) -> c k e", e=P)),
                               (4, 8, a["L0_xattn_Wkv"].rearrange("c (k e) -> c k e", e=P)),
                               (12, 4, a["L0_xattn_Wout"].rearrange("(k e) c -> e k c", e=P))):
                sp.dma_start(wraw[:, at:at + n, :], src).then_inc(S["first_weights_in"], 16)
            small_param(gin[:, 0:2], "g_xattn", "norm_params_in")
            small_param(gin[:, 2:4], "g_ffn", "norm_params_in")
            for dst, src in ((lnmw, "L0_xattn_ln_m_w"), (lnmb, "L0_xattn_ln_m_b"),
                             (lnlw, "L0_xattn_ln_l_w"), (lnlb, "L0_xattn_ln_l_b")):
                small_param(dst[:, :], src, "norm_params_in")
            for at, n, src in ((16, 8, a["L1_xattn_Wq"].rearrange("(k e) c -> e k c", e=P)),
                               (24, 8, a["L1_xattn_Wk"].rearrange("(k e) c -> e k c", e=P)),
                               (32, 8, a["L1_xattn_Wv"].rearrange("(k e) c -> e k c", e=P)),
                               (40, 8, a["L1_xattn_Wo"].rearrange("c (k e) -> c k e", e=P))):
                sp.dma_start(wraw[:, at:at + n, :], src).then_inc(S["weights_in"], 16)
            for s, w in enumerate(("L0_ffn_weight", "L0_ffn_aux_weight1", "L0_ffn_aux_weight2",
                                   "L1_ffn_W_in", "L1_ffn_W_out")):
                sp.dma_start(Wsm[:, s, :], a[w]).then_inc(S["weights_in"], 16)
            sp.dma_start(Wsm[0:E, 5, :], a["L1_ffn_Wr"]).then_inc(S["weights_in"], 16)
            for dst, src in ((fbias, "L0_ffn_bias"), (obias, "L1_xattn_bo"), (innw, "L1_ffn_in_norm_w"),
                             (outnw, "L1_ffn_out_norm_w"), (ebias, "L1_ffn_expert_bias")):
                small_param(dst[:, :], src, "params_in")
            sp.dma_start(enw[:, :, :], a["L1_ffn_enorm_w"].rearrange("(a e) d -> a e d", a=1)
                         .to_broadcast([P, E, C])).then_inc(S["params_in"], 16)

            c = a["ctx_1024"]
            for L in (L0, L1):
                if L is L1:
                    sp.wait_ge(S["values_done"], prepared(L0, LOOPS - 1, 2))
                    sp.wait_ge(S["piece_done"], every.at(L0, LOOPS - 1, len(L0.flat + L0.tail)))
                    load(c[0], 0)
                load(c[1], 1)
                with sp.Fori(0, LOOPS - 1) as i:
                    for par in range(2):
                        sp.wait_ge(S["values_done"], prepared(L, i, par))
                        sp.sem_inc(S["waited"], 1)
                        m = operands_complete(L, 1) if par else 0
                        sp.wait_ge(S["piece_done"], every.at(L, i, m))
                        sp.sem_inc(S["waited"], 1)
                        load(c[bass.ds(2 * i + 2 + par, 1), :, :].rearrange("a k c -> (a k) c"), par)
                sp.wait_ge(S["values_done"], prepared(L, LOOPS - 1, 0))
                sp.wait_ge(S["piece_done"], every.at(L, LOOPS - 1, 0))
                load(c[0], 0)
                if L.lat:
                    sp.wait_ge(S["values_done"], prepared(L, LOOPS - 1, 1))
                    sp.wait_ge(S["piece_done"], every.at(L, LOOPS - 1, operands_complete(L, 1)))
                    load(c[1], 1)

            def load_expert(ep, e):
                for at, src in ((0, a["L1_ffn_Wg"][bass.ds(e, 1)].rearrange("a (k p) d -> p (a k) d", p=P)),
                                (4, a["L1_ffn_Wu"][bass.ds(e, 1)].rearrange("a (k p) d -> p (a k) d", p=P)),
                                (8, a["L1_ffn_Wd"][bass.ds(e, 1)].rearrange("a o (k p) -> o (a k) p", p=P))):
                    at += ep * 3 * FT
                    sp.dma_start(wraw[:, at:at + FT, :], src).then_inc(S[f"moe_in{ep}"], 16)

            sp.wait_ge(S["fold_done"], FOLDS)
            load_expert(0, 0)
            load_expert(1, 1)
            with sp.Fori(0, E // 2 - 1) as i:
                for ep in range(2):
                    sp.wait_ge(S["w_lo"], i * 6 + 3 * (ep + 1))
                    sp.sem_inc(S["waited"], 1)
                    load_expert(ep, 2 * i + 2 + ep)
            sp.wait_ge(S["w_lo"], 3 * (E - 1))
            load_expert(0, 0)
            sp.wait_ge(S["moe_in0"], 48 * (E // 2 + 1))
            sp.wait_ge(S["x_final"], 1)
            sp.dma_start(a["out"].rearrange("b q c -> q b c"), x[:NQ, 1:, :]).then_inc(S["out_in"], 16)
            sp.wait_ge(S["out_in"], 16)

        @block.gpsimd
        def _(pool):
            pool.sem_inc(S["alo_ready"], 1)
            nc.gpsimd.memset(raw[:, :, KT - 1, :], 0.0).then_inc(S["pad_ready"], 1)
            nc.gpsimd.memset(ident[:, :], 0.0).then_inc(S["ident_ready"], 1)
            pool.wait_ge(S["ident_ready"], 1)
            nc.gpsimd.affine_select(out=ident[:, :], in_=ident[:, :], compare_op=ALU.not_equal, fill=1.0, base=0,
                                    pattern=[[-1, P]], channel_multiplier=1).then_inc(S["ident_ready"], 1)
            nc.gpsimd.memset(minus_half[:, :], -0.5)
            for par in range(2):
                nc.gpsimd.memset(Xhi[:, par, KT, :], 0.0)
                nc.gpsimd.memset(Xlo[:, par, KT, :], 0.0)
                nc.gpsimd.memset(prob[:, par, NK:KW], 0.0)
                for L in (L0, L1):
                    nc.gpsimd.memset(QThi[:, par, L.heads * NQ:L.T * P], 0.0)
                    nc.gpsimd.memset(QTlo[:, par, L.heads * NQ:L.T * P], 0.0)
            nc.gpsimd.memset(xq[:, B, :], 0.0)
            nc.gpsimd.memset(xqT[:, B * NQ:], 0.0)
            for e in range(E):
                last = nc.gpsimd.memset(iota8[:, e:e + 1], float(e - E))
            last.then_inc(S["zeros_ready"], 1)

            def prepare(L, i, ahead, bq):
                par = ahead % 2
                X = raw[:, par, :, :]
                done = prepared(L, i, ahead)
                if L.lat:
                    pool.wait_ge(S["stats_ready"], done)
                    nc.gpsimd.tensor_tensor(rstd_k[:, :], var_k[:, :], minus_half[:, 0:KT], ALU.pow).then_inc(S["scaled"], 1)
                    pool.wait_ge(S["scaled"], prepared(L, i, ahead, 3) - 2)
                    pool.sem_inc(S["waited"], 1)
                    for t in range(KT):
                        last = nc.gpsimd.tensor_scalar(raw[:, par, t, :], raw[:, par, t, :], nmean_k[:, t:t + 1],
                                                       rstd_k[:, t:t + 1], ALU.add, ALU.mult)
                    last.then_inc(S["scaled"], 1)
                    pool.wait_ge(S["scaled"], prepared(L, i, ahead, 3) - 1)
                    nc.gpsimd.tensor_tensor(X, X, lnmw[:, :].unsqueeze(1).to_broadcast([P, KT, C]),
                                            ALU.mult).then_inc(S["scaled"], 1)
                    pool.wait_ge(S["scaled"], prepared(L, i, ahead, 3))
                    nc.gpsimd.tensor_tensor(X, X, lnmb[:, :].unsqueeze(1).to_broadcast([P, KT, C]),
                                            ALU.add).then_inc(S["normed"], 1)
                    pool.wait_ge(S["normed"], done)
                pool.wait_ge(S["values_hi"], done)
                last = nc.gpsimd.tensor_tensor(Xlo[:, par, 0:KT, :], X, Xhi[:, par, 0:KT, :], ALU.subtract)
                if L.lat:
                    nc.gpsimd.tensor_tensor(Xlo[:NQ, par, KT, :],
                                            xq[:NQ, bass.ds(bq, 1), :].rearrange("p a c -> p (a c)"),
                                            Xhi[:NQ, par, KT, :], ALU.subtract)
                    last = nc.gpsimd.tensor_tensor(XTlo[:, par, LATC], xqT[:, bass.ds(bq * NQ, NQ)],
                                                   XThi[:, par, LATC], ALU.subtract)
                last.then_inc(S["values_done"], 1)

            def power(n):
                pool.wait_ge(S["var_ready"], n)
                nc.gpsimd.tensor_tensor(small[:NQ, 2, :], small[:NQ, 1, :], minus_half[:NQ, :],
                                        ALU.pow).then_inc(S["rstd_ready"], 1)

            pool.wait_ge(S["zeros_ready"], 1)
            power(1)
            power(2)
            pool.wait_ge(S["norm_params_in"], 16 * NORM_PARAMS)
            for L in (L0, L1):
                if L is L1:
                    power(3)
                    power(4)
                prepare(L, 0, 0, 0)
                with pool.Fori(0, LOOPS) as i:
                    prepare(L, i, 1, 2 * i + 1)
                    prepare(L, i, 2, 2 * i + 2)

            power(5)
            power(6)
            with pool.Fori(0, E // 2) as i:
                for J in range(CHUNKS + 2):
                    for f in range(FT):
                        if J < CHUNKS:
                            u = J * FT + f
                            pool.wait_ge(S["ahi_ready"], i * UNITS + u + 1)
                            nc.gpsimd.tensor_tensor(alo[:, J % 2, f, :], actf[:, u % 2, :], ahi[:, J % 2, f, :],
                                                    ALU.subtract).then_inc(S["alo_ready"], 1)
                        if J >= 2 and f == 2:
                            d = J % 2
                            pool.wait_ge(S["ms_ready"], i * CHUNKS + J - 1)
                            nc.gpsimd.tensor_tensor(coef[:NQ, d, 1, :], coef[:NQ, d, 0, :], minus_half[:NQ, 0:GROUP],
                                                    ALU.pow).then_inc(S["coef_ready"], 1)
            power(7)

        @block.tensor
        def _(pe):
            mm, tr = nc.tensor.matmul, nc.tensor.transpose
            pe.sem_inc(S["v_ready"], 1)
            pe.sem_inc(S["down_ready"], 2)

            pe.wait_ge(S["ident_ready"], 2)
            pe.wait_ge(S["first_weights_in"], 16 * FIRST_WEIGHTS)
            for n, group in enumerate(FOLD):
                if n == FIRST_FOLDS:
                    pe.wait_ge(S["weights_in"], 16 * WEIGHTS)
                if n >= 4:
                    pe.wait_ge(S["fold_done"], n - 3)
                needs, _, _, members = group
                if needs:
                    pe.wait_ge(S["fold_done"], needs)
                for s, (l, r) in enumerate(members):
                    o = score[:, n % 4, s * P:(s + 1) * P]
                    last = tr(o, l, ident[:, :]) if r is None else mm(o, l, r, start=True, stop=True)
                last.then_inc(S["fold_ready"], 1)
            for s, m in enumerate((0, 3, 4)):
                tr(side[:, s * P:(s + 1) * P], Wsm[:, m, :], ident[:, :])
            tr(side[:, 3 * P:3 * P + E], Wsm[0:E, 5, :], ident[0:E, 0:E]).then_inc(S["small_ready"], 1)
            pe.wait_ge(S["small_done"], 1)
            mm(side[:, 0:P], Wsm[:, 1, :], WsmT[:, 0, :], start=True, stop=True).then_inc(S["small_ready"], 1)
            pe.wait_ge(S["small_done"], 2)
            mm(side[:, 0:P], Wf[:, 0, :], Wsm[:, 2, :], start=True, stop=True).then_inc(S["small_ready"], 1)
            pe.wait_ge(S["small_done"], 3)

            def glue_transposes(n):
                for k in range(GLUE):
                    pe.wait_ge(S["xq_ready"], n * GLUE + k + 1)
                    for s in range(GROUP):
                        b = k * GROUP + s
                        last = tr(score[:, k, s * NQ:(s + 1) * NQ], xq[:NQ, b, :], ident[:NQ, :NQ])
                    last.then_inc(S["glue_T_ready"], 1)

            pe.wait_ge(S["fold_done"], FOLDS)
            glue_transposes(0)
            pe.wait_ge(S["null_ready"], 1)
            pe.wait_ge(S["glue_T_done"], GLUE)

            def attention(L, glue=None):
                A0 = 0 if L.lat else L0.heads

                def piece(i, idx, kind, par, k, bq):
                    pe.wait_ge(S["piece_done"], idx)
                    if kind == "Q":
                        for s in range(GROUP):
                            last = mm(side[:, s * NQ:(s + 1) * NQ], Amat[:, A0 + k * GROUP + s, :],
                                      xqT[:, bass.ds(bq * NQ, NQ)] if i is not None else xqT[:, 0:NQ],
                                      start=True, stop=True)
                    elif kind == "X":
                        for s in range(GROUP):
                            last = tr(side[:, s * P:(s + 1) * P], raw[:, par, k * GROUP + s, :], ident[:, :])
                    elif kind == "Z":
                        last = tr(side[:, 0:P], Zs[:, k, :], ident[:, :])
                    else:
                        for h in range(L.heads):
                            last = mm(side[:NQ, 0:C], ZT[:, par, h * NQ:(h + 1) * NQ], Mmat[:, A0 + h, :],
                                      start=(h == 0), stop=(h == L.heads - 1))
                    last.then_inc(S["piece_ready"], 1)

                for m, (kind, par, k) in enumerate(L.prologue):
                    if m == L.glue_at:
                        glue()
                    if kind == "X":
                        if L.lat:
                            pe.wait_ge(S["normed"], prepared(L, 0, 0))
                        else:
                            pe.wait_ge(S["ctx_in0"], loaded(L, 0, 0))
                    piece(None, every.prologue(L, m), kind, par, k, 0)

                def scores(i, n, c):
                    bp, t = n // L.T, n % L.T
                    if t == 0 and c == 0:
                        m = operands_complete(L, 1) if bp else 0
                        pe.wait_ge(S["piece_done"], every.at(L, i, m))
                        pe.wait_ge(S["values_done"], prepared(L, i, bp))
                    if c % 2 == 0:
                        pe.wait_ge(S["score_copied"], copied_c.at(L, i, n - 1, c // 2 + 1))
                    qh, ql = (w[:, bp, t * P:(t + 1) * P] for w in (QThi, QTlo))
                    parts = [(slice(0, CH), slice(c * CH, (c + 1) * CH))]
                    if L.lat and c == 3:
                        parts.append((slice(CH, CH + NQ), LATC))
                    for o, s in parts:
                        out = score[:, c, o]
                        mm(out, qh, XThi[:, bp, s], start=True, stop=False)
                        mm(out, qh, XTlo[:, bp, s], start=False, stop=False)
                        last = mm(out, ql, XThi[:, bp, s], start=False, stop=True)
                    if c % 2:
                        last.then_inc(S["score_ready"], 1)

                def turn_group(i, n, k):
                    pe.wait_ge(S["exp_done"], exp_c.at(L, i, n))
                    pe.wait_ge(S["pt_lo"], ptlo_c.at(L, i, n, k - 1))
                    for s in range(min(GROUP, L.KT - k * GROUP)):
                        kt = k * GROUP + s
                        last = tr(turn[:, (n * L.groups + k) % 2, s * P:(s + 1) * P],
                                  prob[:, (n - 1) % 2, kt * P:(kt + 1) * P], ident[:, :])
                    last.then_inc(S["turned"], 1)

                def values(i, n, kts):
                    q, vp = n % 2, (n - 2) // L.T % 2
                    if kts[0] == 0:
                        pe.wait_ge(S["z_scaled"], z_c.at(L, i, n))
                        pe.wait_ge(S["pt_lo"], ptlo_c.at(L, i, n))
                    for kt in kts:
                        ph, pl = (w[:, q, kt * P:(kt + 1) * P] for w in (PThi, PTlo))
                        mm(vbank[:, 0:C], ph, Xhi[:, vp, kt, :], start=(kt == 0), stop=False)
                        mm(vbank[:, 0:C], ph, Xlo[:, vp, kt, :], start=False, stop=False)
                        last = mm(vbank[:, 0:C], pl, Xhi[:, vp, kt, :], start=False, stop=(kt == L.KT - 1))
                    if kts[-1] == L.KT - 1:
                        last.then_inc(S["v_ready"], 1)

                def step(i, n, m):
                    cuts = [range(0, 4), range(4, 9), range(9, L.KT)]
                    for c in range(4):
                        if n < L.N:
                            scores(i, n, c)
                        if n <= L.N and c % 2:
                            turn_group(i, n, c // 2)
                        if c == 1:
                            pe.wait_ge(S["z_scaled"], z_c.at(L, i, n))
                            piece(i, every.at(L, i, m), "Z", None, (n - 3) % 2, None)
                    if n <= L.N + 1:
                        values(i, n, cuts[0])
                    if n <= L.N:
                        for k in range(2, L.early):
                            turn_group(i, n, k)
                    for kind, par, k in L.sched[n][1:]:
                        m += 1
                        if kind == "X":
                            if L.lat:
                                pe.wait_ge(S["normed"], prepared(L, i, 2 - par))
                            else:
                                pe.wait_ge(S[f"ctx_in{par}"], loaded(L, i, 2 - par))
                        piece(i, every.at(L, i, m), kind, par, k, 2 * i + (2 - par) if kind == "Q" else None)
                    if n <= L.N + 1:
                        values(i, n, cuts[1])
                    if n <= L.N:
                        for k in range(L.early, L.groups):
                            turn_group(i, n, k)
                    if n <= L.N + 1:
                        values(i, n, cuts[2])
                    return m + 1

                with pe.Fori(0, LOOPS) as i:
                    m = 0
                    for n in range(L.N):
                        m = step(i, n, m)
                for n in range(L.N, L.N + 3):
                    m = step(LOOPS - 1, n, m)

            attention(L0)

            def token_matmul(weights):
                for k in range(GLUE):
                    for s in range(GROUP):
                        b = k * GROUP + s
                        last = mm(score[:NQ, k, s * P:(s + 1) * P], xqT[:, b * NQ:(b + 1) * NQ], weights,
                                  start=True, stop=True)
                    last.then_inc(S["token_mm"], 1)

            def dense_ffn():
                glue_transposes(1)
                pe.wait_ge(S["glue_T_done"], 2 * GLUE)
                token_matmul(Wf[:, 1, :])
                glue_transposes(2)
                pe.wait_ge(S["glue_T_done"], 3 * GLUE)

            attention(L1, dense_ffn)

            def turn_weights(ep, k, value, arrived):
                pe.wait_ge(S[f"moe_in{ep}"], arrived)
                pe.wait_ge(S["w_lo"], value)
                for s in range(FT):
                    last = tr(side[:, s * P:(s + 1) * P], wraw[:, (ep * 3 + k) * FT + s, :], ident[:, :])
                last.then_inc(S["w_turned"], 1)

            pe.wait_ge(S["piece_done"], every.at(L1, LOOPS - 1, len(L1.flat + L1.tail)))
            turn_weights(0, 0, 0, 48)
            turn_weights(0, 1, 1, 48)
            glue_transposes(3)
            pe.wait_ge(S["glue_T_done"], 4 * GLUE)
            token_matmul(WsmT[:, 1, :])
            turn_weights(0, 2, 2, 48)
            glue_transposes(4)
            pe.wait_ge(S["glue_T_done"], 5 * GLUE)
            for b in range(B):
                last = mm(vbank[:NQ, b * E:(b + 1) * E], xqT[:, b * NQ:(b + 1) * NQ], WsmT[:, 3, 0:E],
                          start=True, stop=True)
            last.then_inc(S["logits_ready"], 1)

            pe.wait_ge(S["h_split"], 1)
            with pe.Fori(0, E // 2) as i:
                for J in range(CHUNKS + 1):
                    for f in range(FT):
                        if J < CHUNKS:
                            ep, j, u = J // 4, J % 4, J * FT + f
                            if u % (4 * FT) == 0:
                                pe.wait_ge(S["w_lo"], i * 6 + 3 * ep + 3)
                            pe.wait_ge(S["act_ready"], i * UNITS + u + 1)
                            cols = slice(j * 4 * NQ, (j + 1) * 4 * NQ)
                            for w in range(2):
                                out = score[:, (u % 2) * 2 + w, 0:4 * NQ]
                                wh, wl = (v[:, ep, w, f * P:(f + 1) * P] for v in (wThi, wTlo))
                                mm(out, wh, hThi[:, cols], start=True, stop=False)
                                mm(out, wh, hTlo[:, cols], start=False, stop=False)
                                last = mm(out, wl, hThi[:, cols], start=False, stop=True)
                            last.then_inc(S["gu_ready"], 1)
                        for s in ((), (0,), (1,), (2, 3))[f] if J >= 1 else ():
                            D = J - 1
                            ep = D // 4
                            if s == 0:
                                pe.wait_ge(S["alo_ready"], i * UNITS + D * FT + FT + 1)
                                pe.wait_ge(S["down_copied"], i * CHUNKS + D + 1)
                            toks = slice(s * NQ, (s + 1) * NQ)
                            out = turn[:NQ, D % 2, s * P:(s + 1) * P]
                            for g in range(FT):
                                dh, dl = (v[:, ep, 2, g * P:(g + 1) * P] for v in (wThi, wTlo))
                                ah, al = (v[:, D % 2, g, toks] for v in (ahi, alo))
                                mm(out, ah, dh, start=(g == 0), stop=False)
                                mm(out, ah, dl, start=False, stop=False)
                                last = mm(out, al, dh, start=False, stop=(g == FT - 1))
                            if s == GROUP - 1:
                                last.then_inc(S["down_ready"], 1)
                    if J < CHUNKS and J % 4 < 3:
                        ep, k = J // 4, J % 4
                        turn_weights(1 - ep, k, i * 6 + 3 * (ep + 1) + k, (i + 1 + ep) * 48)
            glue_transposes(5)
            pe.wait_ge(S["glue_T_done"], 6 * GLUE)
            token_matmul(WsmT[:, 2, :])

        @block.scalar
        def _(act):
            fn = nc.scalar.activation
            act.sem_inc(S["exp_done"], 1)
            act.sem_inc(S["z_scaled"], 1)
            act.sem_inc(S["down_copied"], 2)
            act.wait_ge(S["norm_params_in"], 16 * NORM_PARAMS)
            fn(gt[:, :], gin[:, :], ACT.Tanh).then_inc(S["gates_tanh"], 1)
            act.wait_ge(S["gates_tanh"], 1)
            for n, group in enumerate(FOLD):
                act.wait_ge(S["fold_ready"], n + 1)
                _, dst, scale, _ = group
                src = score[:, n % 4, :].rearrange("p (s c) -> p s c", c=P)
                fn(dst, src, ACT.Copy, scale=scale).then_inc(S["fold_done"], 1)
            act.wait_ge(S["small_ready"], 1)
            fn(WsmT[:, 0:3, :], side[:, 0:3 * P].rearrange("p (s c) -> p s c", c=P), ACT.Copy)
            fn(WsmT[:, 3, 0:E], side[:, 3 * P:3 * P + E], ACT.Copy).then_inc(S["small_done"], 1)
            for s in range(2):
                act.wait_ge(S["small_ready"], 2 + s)
                fn(Wf[:, s, :], side[:, 0:P], ACT.Copy).then_inc(S["small_done"], 1)

            def glue_copies(n):
                for k in range(GLUE):
                    act.wait_ge(S["glue_T_ready"], n * GLUE + k + 1)
                    fn(xqT[:, qcols(k)], score[:, k, 0:GROUP * NQ], ACT.Copy).then_inc(S["glue_T_done"], 1)

            glue_copies(0)
            act.wait_ge(S["glue_T_done"], GLUE)
            act.wait_ge(S["null_ready"], 1)

            def attention(L, glue=None):
                def split_hi(kind, par, k, value):
                    act.wait_ge(S["piece_ready"], value)
                    if kind == "Q":
                        fn(QThi[:, par, qcols(k)], side[:, 0:GROUP * NQ], ACT.Copy).then_inc(S["piece_hi"], 1)
                    else:
                        cols = slice(k * GROUP * P, (k + 1) * GROUP * P)
                        fn(XThi[:, par, cols], side[:, :], ACT.Copy).then_inc(S["piece_hi"], 1)

                def values_hi(i, ahead, bq):
                    par = ahead % 2
                    if L.lat:
                        act.wait_ge(S["normed"], prepared(L, i, ahead))
                        fn(Xhi[:NQ, par, KT, :], xq[:NQ, bass.ds(bq, 1), :].rearrange("p a c -> p (a c)"), ACT.Copy)
                        fn(XThi[:, par, LATC], xqT[:, bass.ds(bq * NQ, NQ)], ACT.Copy)
                    else:
                        act.wait_ge(S[f"ctx_in{par}"], loaded(L, i, ahead))
                    fn(Xhi[:, par, 0:KT, :], raw[:, par, :, :], ACT.Copy).then_inc(S["values_hi"], 1)

                act.wait_ge(S["zeros_ready"], 1)
                for m, (kind, par, k) in enumerate(L.prologue):
                    if m == L.glue_at:
                        values_hi(0, 0, 0)
                        glue()
                    if L.lat and m == L.qgroups:
                        values_hi(0, 0, 0)
                    split_hi(kind, par, k, every.prologue(L, m) + 1)

                def step(i, n, m):
                    def pt_hi(groups):
                        for k in groups:
                            act.wait_ge(S["turned"], turned_c.at(L, i, n, k + 1))
                            if k == 0:
                                act.wait_ge(S["v_ready"], v_c.at(L, i, n))
                            w = min(GROUP, L.KT - k * GROUP) * P
                            fn(PThi[:, (n - 1) % 2, k * GROUP * P:k * GROUP * P + w],
                               turn[:, (n * L.groups + k) % 2, 0:w], ACT.Copy).then_inc(S["pt_hi"], 1)

                    if n <= L.N:
                        pt_hi(range(L.early))
                    for kind, par, k in L.sched[n]:
                        if kind in "QX":
                            split_hi(kind, par, k, every.at(L, i, m) + 1)
                        m += 1
                    if n < L.N:
                        p = n % 2
                        act.wait_ge(S["negm_ready"], negm_c.at(L, i, n, 1))
                        for s, cols in enumerate((slice(0, NK), LATC)[:L.sums]):
                            last = fn(prob[:, p, cols], prob[:, p, cols], ACT.Exp, bias=negm[:, p:p + 1],
                                      accum_out=lsum[:, p, s:s + 1])
                        last.then_inc(S["exp_done"], 1)
                    if n <= L.N:
                        pt_hi(range(L.early, L.groups))
                    if n <= L.N + 1:
                        act.wait_ge(S["v_ready"], v_c.at(L, i, n, 1))
                        act.wait_ge(S["rinv_ready"], rinv_c.at(L, i, n))
                        fn(Zs[:, n % 2, :], vbank[:, 0:C], ACT.Copy, scale=rinv[:, n % 2:n % 2 + 1]).then_inc(S["z_scaled"], 1)
                    if n < L.N and n % L.T == L.values_at:
                        ahead = n // L.T + 1
                        values_hi(i, ahead, 2 * i + ahead)
                    return m

                with act.Fori(0, LOOPS) as i:
                    m = 0
                    for n in range(L.N):
                        m = step(i, n, m)
                for n in range(L.N, L.N + 3):
                    m = step(LOOPS - 1, n, m)

            def dense_ffn():
                glue_copies(1)
                for k in range(GLUE):
                    part = tmp[:NQ, k * GROUP:(k + 1) * GROUP, :]
                    act.wait_ge(S["ffn_biased"], k + 1)
                    fn(part, part, ACT.Tanh).then_inc(S["ffn_tanh"], 1)
                glue_copies(2)

            attention(L0)
            attention(L1, dense_ffn)

            def weights_hi(ep, k, value):
                act.wait_ge(S["w_turned"], value)
                fn(wThi[:, ep, k, :], side[:, :], ACT.Copy, scale=WSCALE).then_inc(S["w_hi"], 1)

            weights_hi(0, 0, 1)
            weights_hi(0, 1, 2)
            glue_copies(3)
            weights_hi(0, 2, 3)
            glue_copies(4)
            act.wait_ge(S["glue_T_done"], 5 * GLUE)
            fn(hThi[:, 0:B * NQ], xqT[:, 0:B * NQ], ACT.Copy).then_inc(S["h_hi"], 1)
            act.wait_ge(S["route_ready"], 1)
            fn(route[:NQ, 5, :], route[:NQ, 4, :], ACT.Exp).then_inc(S["route_exp"], 1)

            with act.Fori(0, E // 2) as i:
                for J in range(CHUNKS + 2):
                    for f in range(FT):
                        if J < CHUNKS:
                            u = J * FT + f
                            act.wait_ge(S["gu_ready"], i * UNITS + u + 1)
                            fn(sil[:, u % 2, :], score[:, (u % 2) * 2, 0:4 * NQ], ACT.Silu,
                               scale=1.0 / WSCALE).then_inc(S["sil_ready"], 1)
                        if J >= 2 and f < 2:
                            D = J - 2
                            if f == 0:
                                act.wait_ge(S["down_ready"], i * CHUNKS + D + 3)
                                act.wait_ge(S["acc_ready"], i * CHUNKS + D + 1)
                                fn(dsb[:NQ, D % 2, :, :], turn[:NQ, D % 2, :].rearrange("p (s c) -> p s c", c=C),
                                   ACT.Copy).then_inc(S["down_copied"], 1)
                                act.wait_ge(S["down_copied"], i * CHUNKS + D + 3)
                            for s in (2 * f, 2 * f + 1):
                                last = fn(sqs[:NQ, D % 2, s, :], dsb[:NQ, D % 2, s, :], ACT.Square,
                                          scale=1.0 / WSCALE ** 2, accum_out=ssq[:NQ, D % 2, s:s + 1])
                            if f == 1:
                                last.then_inc(S["sq_ready"], 1)
                    if J < CHUNKS and J % 4 < 3:
                        ep, k = J // 4, J % 4
                        weights_hi(1 - ep, k, i * 6 + 3 * (ep + 1) + k + 1)
            glue_copies(5)

        @block.vector
        def _(dve):
            v = nc.vector
            chain, norms = [0], [0]

            def link(ins):
                chain[0] += 1
                ins.then_inc(S["dve_chain"], 1)
                dve.wait_ge(S["dve_chain"], chain[0])

            dve.sem_inc(S["pt_lo"], 2)
            dve.sem_inc(S["score_copied"], 2)
            dve.sem_inc(S["rinv_ready"], 1)
            dve.sem_inc(S["act_ready"], 2)
            dve.sem_inc(S["acc_ready"], 2)

            def over(vec):
                return vec.unsqueeze(1).to_broadcast([NQ, B, C])

            s1, s2, s3, s4 = (small[:NQ, k, :] for k in (1, 2, 3, 4))
            mean, var = mvx[:NQ, :, 0], mvx[:NQ, :, 1]

            def norm_stats(src, before):
                for k in range(GLUE):
                    before(k)
                    for b in range(k * GROUP, (k + 1) * GROUP):
                        last = v.bn_stats(stat6[:NQ, b, :], src(b))
                link(last)
                for b in range(B):
                    last = v.bn_aggr(mvx[:NQ, b, :], stat6[:NQ, b, :])
                link(last)

            def ask_power(ins):
                ins.then_inc(S["var_ready"], 1)
                norms[0] += 1

            def apply(src, scale, weight=None):
                for k in range(GLUE):
                    for b in range(k * GROUP, (k + 1) * GROUP):
                        if weight is None:
                            last = v.tensor_scalar(xq[:NQ, b, :], src(b), mvx[:NQ, b, 0:1], scale[:, b:b + 1],
                                                   ALU.subtract, ALU.mult)
                        else:
                            last = v.scalar_tensor_tensor(out=xq[:NQ, b, :], in0=src(b), scalar=scale[:, b:b + 1],
                                                          in1=weight[:NQ, :], op0=ALU.mult, op1=ALU.mult)
                    last.then_inc(S["xq_ready"], 1)

            def layer_norm(src, before=lambda k: None, meanwhile=lambda: None):
                norm_stats(src, before)
                ask_power(v.tensor_scalar(s1, var, LN_EPS, None, ALU.add))
                meanwhile()
                dve.wait_ge(S["rstd_ready"], norms[0])
                apply(src, s2)

            def rms_norm(src, weight, before=lambda k: None, meanwhile=lambda: None):
                norm_stats(src, before)
                link(v.tensor_tensor(s3, mean, mean, ALU.mult))
                ask_power(v.scalar_tensor_tensor(out=s1, in0=var, scalar=RMS_EPS, in1=s3, op0=ALU.add, op1=ALU.add))
                meanwhile()
                dve.wait_ge(S["rstd_ready"], norms[0])
                apply(src, s2, weight)

            def row_stats(L, i, ahead, part):
                par = ahead % 2
                if part == 0:
                    dve.wait_ge(S[f"ctx_in{par}"], loaded(L, i, ahead))
                for t in range(5 * part, min(5 * part + 5, KT)):
                    last = v.bn_stats(stat6[:, t, :], raw[:, par, t, :])
                if part == 2:
                    last.then_inc(S["stat_step"], 1)

            def stats(L, i, ahead):
                done = prepared(L, i, ahead)
                dve.wait_ge(S["stat_step"], prepared(L, i, ahead, 2) - 1)
                dve.sem_inc(S["waited"], 1)
                for t in range(KT):
                    last = v.bn_aggr(mv[:, t, :], stat6[:, t, :])
                last.then_inc(S["stat_step"], 1)
                dve.wait_ge(S["stat_step"], prepared(L, i, ahead, 2))
                dve.wait_ge(S["normed"], done - 1)
                v.tensor_scalar(nmean_k[:, :], mv[:, :, 0], -1.0, None, ALU.mult)
                v.tensor_scalar(var_k[:, :], mv[:, :, 1], LN_EPS, None, ALU.add).then_inc(S["stats_ready"], 1)

            xv = x[:NQ, 1:, :]

            def latents(b):
                return x[:NQ, b + 1, :]

            dve.wait_ge(S["x_in"], 16)
            norm_stats(latents, lambda k: None)
            ask_power(v.tensor_scalar(s1, var, LN_EPS, None, ALU.add))
            for part in range(3):
                row_stats(L0, 0, 0, part)
            dve.wait_ge(S["rstd_ready"], 1)
            link(v.tensor_copy(s4, s2))
            link(v.tensor_tensor(s3, var, s4, ALU.mult))
            link(v.tensor_tensor(s3, s3, s4, ALU.mult))
            ask_power(v.tensor_scalar(s1, s3, LN_EPS, None, ALU.add))
            stats(L0, 0, 0)
            dve.wait_ge(S["rstd_ready"], 2)
            link(v.tensor_tensor(s3, s2, s4, ALU.mult))
            dve.wait_ge(S["norm_params_in"], 16 * NORM_PARAMS)
            for b in range(B):
                last = v.tensor_scalar(xq[:NQ, b, :], latents(b), mvx[:NQ, b, 0:1], s3[:, b:b + 1],
                                       ALU.subtract, ALU.mult)
            link(last)
            for k in range(GLUE):
                part = xq[:NQ, k * GROUP:(k + 1) * GROUP, :]
                wk, bk = (w[:NQ, :].unsqueeze(1).to_broadcast([NQ, GROUP, C]) for w in (lnlw, lnlb))
                link(v.tensor_tensor(part, part, wk, ALU.mult))
                v.tensor_tensor(part, part, bk, ALU.add).then_inc(S["xq_ready"], 1)
            v.memset(prob[:, 1, 0:NK], 0.0)
            v.memset(Xhi[:, 1, 0:KT, :], 0.0)
            v.memset(Xlo[:, 1, 0:KT, :], 0.0)
            v.memset(PThi[:, 0, :], 0.0)
            v.memset(PTlo[:, 0, :], 0.0)
            v.memset(ZT[:, 1, :], 0.0)
            v.memset(Zs[:, :, :], 0.0)
            v.memset(x[:, 0, :], 0.0)
            v.memset(rinv[:, :], 1.0)
            v.memset(lsum[:, :, :], 1.0).then_inc(S["null_ready"], 1)
            dve.wait_ge(S["zeros_ready"], 1)
            row_stats(L0, 0, 1, 0)
            dve.wait_ge(S["params_in"], 16 * PARAMS)
            dve.wait_ge(S["gates_tanh"], 1)
            link(v.tensor_scalar(obias[:, :], obias[:, :], gt[:, 1:2], None, ALU.mult))

            def attention(L, glue=None):
                def split_lo(kind, par, k, value):
                    dve.wait_ge(S["piece_hi"], value)
                    if kind == "Q":
                        v.tensor_tensor(QTlo[:, par, qcols(k)], side[:, 0:GROUP * NQ], QThi[:, par, qcols(k)],
                                        ALU.subtract).then_inc(S["piece_done"], 1)
                    else:
                        cols = slice(k * GROUP * P, (k + 1) * GROUP * P)
                        v.tensor_tensor(XTlo[:, par, cols], side[:, :], XThi[:, par, cols],
                                        ALU.subtract).then_inc(S["piece_done"], 1)

                def first_lo(m):
                    kind, par, k = L.prologue[m]
                    split_lo(kind, par, k, split.prologue(L, m) + 1)

                if glue:
                    glue(first_lo)
                for m in range(L.glue_at or 0, len(L.prologue)):
                    first_lo(m)
                if L is L1:
                    dve.wait_ge(S["xq_ready"], 3 * GLUE)
                    link(v.tensor_tensor(xv, xv, over(obias[:NQ, :]), ALU.add))

                def copy_max(n, banks, cols, part):
                    out = prob[:, n % 2, cols]
                    if len(banks.shape) == 3:
                        out = out.rearrange("p (b c) -> p b c", b=2)
                    return v.tensor_scalar(out, banks, 1.0, None, ALU.mult, ALU.max, accum_out=mx[:, n % 2, part:part + 1])

                def pt_lo(i, n, k):
                    dve.wait_ge(S["pt_hi"], pthi_c.at(L, i, n, k + 1))
                    w = min(GROUP, L.KT - k * GROUP) * P
                    out = slice(k * GROUP * P, k * GROUP * P + w)
                    v.tensor_tensor(PTlo[:, (n - 1) % 2, out], turn[:, (n * L.groups + k) % 2, 0:w],
                                    PThi[:, (n - 1) % 2, out], ALU.subtract).then_inc(S["pt_lo"], 1)

                def step(i, n, m):
                    p, q = n % 2, (n - 1) % 2
                    if n < L.N:
                        dve.wait_ge(S["score_ready"], score_c.at(L, i, n, 1))
                        copy_max(n, score[:, 0:2, 0:CH], slice(0, 2 * CH), 0).then_inc(S["score_copied"], 1)
                    _, par, k = L.sched[n][0]
                    dve.wait_ge(S["piece_ready"], every.at(L, i, m) + 1)
                    v.tensor_copy(ZT[:, par, k * P:(k + 1) * P], side[:, 0:P]).then_inc(S["piece_done"], 1)
                    if n <= L.N:
                        pt_lo(i, n, 0)
                    if n < L.N:
                        dve.wait_ge(S["score_ready"], score_c.at(L, i, n, 2))
                        last = copy_max(n, score[:, 2:4, 0:CH], slice(2 * CH, NK), 1)
                        if L.lat:
                            last = copy_max(n, score[:, 3, CH:CH + NQ], LATC, 2)
                        last.then_inc(S["score_copied"], 1)
                        dve.wait_ge(S["score_copied"], copied_c.at(L, i, n, 2))
                        v.reduce_max(negm[:, p:p + 1], mx[:, p, 0:L.maxes], AX.X, negate=True).then_inc(S["negm_ready"], 1)
                    if n <= L.N:
                        for k in range(1, L.early):
                            pt_lo(i, n, k)
                    for kind, par, k in L.sched[n][1:]:
                        m += 1
                        if kind in "QX":
                            split_lo(kind, par, k, split.at(L, i, m) + 1)
                        else:
                            dve.wait_ge(S["piece_ready"], every.at(L, i, m) + 1)
                            xb = x[:NQ, bass.ds(2 * i + k, 1), :].rearrange("p a c -> p (a c)")
                            v.tensor_tensor(xb, side[:NQ, 0:C], xb, ALU.add).then_inc(S["piece_done"], 1)
                    if n <= L.N:
                        dve.wait_ge(S["z_scaled"], z_c.at(L, i, n))
                        dve.wait_ge(S["exp_done"], exp_c.at(L, i, n))
                        src = lsum[:, q, 0:1]
                        if L.sums > 1:
                            v.tensor_tensor(lall[:, q:q + 1], lsum[:, q, 0:1], lsum[:, q, 1:2], ALU.add).then_inc(S["sum_ready"], 1)
                            dve.wait_ge(S["sum_ready"], i * L.N + (n + 1))
                            src = lall[:, q:q + 1]
                        v.reciprocal(rinv[:, q:q + 1], src).then_inc(S["rinv_ready"], 1)
                        if L.lat and n < L.N:
                            t, ahead = n % L.T, n // L.T + 1
                            if t < 2:
                                row_stats(L, i, ahead, t + 1)
                            if t == 1:
                                stats(L, i, ahead)
                            if t == L.T - 1:
                                row_stats(L, i, ahead + 1, 0)
                        for k in range(L.early, L.groups):
                            pt_lo(i, n, k)
                    return m + 1

                with dve.Fori(0, LOOPS) as i:
                    m = 0
                    for n in range(L.N):
                        m = step(i, n, m)
                for n in range(L.N, L.N + 3):
                    m = step(LOOPS - 1, n, m)

            attention(L0)
            dve.wait_ge(S["piece_done"], every.at(L0, LOOPS - 1, len(L0.flat + L0.tail)))
            dve.wait_ge(S["values_done"], prepared(L0, LOOPS - 1, 2))

            def dense_ffn(first_lo):
                def two_lo():
                    first_lo(0)
                    first_lo(1)

                layer_norm(latents, meanwhile=two_lo)
                first_lo(2)
                for k in range(GLUE):
                    part = tmp[:NQ, k * GROUP:(k + 1) * GROUP, :]
                    dve.wait_ge(S["token_mm"], k + 1)
                    ps = score[:NQ, k, :].rearrange("p (s c) -> p s c", c=C)
                    v.tensor_tensor(part, ps, fbias[:NQ, :].unsqueeze(1).to_broadcast([NQ, GROUP, C]),
                                    ALU.add).then_inc(S["ffn_biased"], 1)

                def ffn_out(k):
                    part = tmp[:NQ, k * GROUP:(k + 1) * GROUP, :]
                    xk = xv[:, k * GROUP:(k + 1) * GROUP, :]
                    dve.wait_ge(S["ffn_tanh"], k + 1)
                    link(v.scalar_tensor_tensor(out=xk, in0=part, scalar=gt[:NQ, 2:3], in1=xk, op0=ALU.mult, op1=ALU.add))

                layer_norm(latents, ffn_out)

            attention(L1, dense_ffn)
            dve.wait_ge(S["piece_done"], every.at(L1, LOOPS - 1, len(L1.flat + L1.tail)))

            def weights_lo(ep, k, value):
                dve.wait_ge(S["w_hi"], value)
                v.scalar_tensor_tensor(out=wTlo[:, ep, k, :], in0=side[:, :], scalar=WSCALE, in1=wThi[:, ep, k, :],
                                       op0=ALU.mult, op1=ALU.subtract).then_inc(S["w_lo"], 1)

            layer_norm(latents, meanwhile=lambda: weights_lo(0, 0, 1))
            weights_lo(0, 1, 2)
            rms_norm(lambda b: score[:NQ, b // GROUP, b % GROUP * C:(b % GROUP + 1) * C], innw,
                     lambda k: dve.wait_ge(S["token_mm"], GLUE + k + 1), meanwhile=lambda: weights_lo(0, 2, 3))
            dve.wait_ge(S["h_hi"], 1)
            v.tensor_tensor(hTlo[:, 0:B * NQ], xqT[:, 0:B * NQ], hThi[:, 0:B * NQ], ALU.subtract).then_inc(S["h_split"], 1)

            R = [route[:NQ, k, :].rearrange("p (b e) -> p b e", e=E) for k in range(8)]
            st = [small[:NQ, k, :] for k in range(8)]

            def each(s):
                return s.unsqueeze(2).to_broadcast([NQ, B, E])

            io = iota8[:NQ, :].unsqueeze(1).to_broadcast([NQ, B, E])
            dve.wait_ge(S["logits_ready"], 1)
            link(v.tensor_copy(R[0], vbank[:NQ, 0:B * E].rearrange("p (b e) -> p b e", e=E)))
            link(v.tensor_tensor(R[1], R[0], ebias[:NQ, :].unsqueeze(1).to_broadcast([NQ, B, E]), ALU.add))
            for pick in (2, 3):
                link(v.reduce_max(st[0], R[1], AX.X))
                link(v.tensor_tensor(R[6], R[1], each(st[0]), ALU.is_equal))
                link(v.tensor_tensor(R[7], R[6], io, ALU.mult))
                link(v.tensor_reduce(st[1], R[7], AX.X, ALU.min))
                link(v.tensor_tensor(R[pick], io, each(st[1]), ALU.is_equal))
                link(v.scalar_tensor_tensor(out=R[1], in0=R[pick], scalar=-3.0e38, in1=R[1], op0=ALU.mult, op1=ALU.add))
            link(v.tensor_tensor(R[2], R[2], R[3], ALU.add))
            link(v.tensor_scalar(R[3], R[2], -1.0, 3.0e38, ALU.add, ALU.mult))
            link(v.tensor_tensor(R[3], R[3], R[0], ALU.add))
            link(v.reduce_max(st[0], R[3], AX.X))
            link(v.tensor_tensor(R[6], R[0], each(st[0]), ALU.subtract))
            link(v.tensor_tensor(R[6], R[6], R[2], ALU.mult))
            v.tensor_copy(R[4], R[6]).then_inc(S["route_ready"], 1)
            dve.wait_ge(S["route_exp"], 1)
            link(v.tensor_tensor(R[5], R[5], R[2], ALU.mult))
            link(v.reduce_sum(st[0], R[5], AX.X))
            link(v.reciprocal(st[1], st[0]))
            link(v.tensor_tensor(R[0], R[5], each(st[1]), ALU.mult))
            link(v.memset(tmp[:NQ, :, :], 0.0))

            with dve.Fori(0, E // 2) as i:
                for J in range(CHUNKS + 3):
                    for f in range(FT):
                        if J < CHUNKS:
                            u = J * FT + f
                            dve.wait_ge(S["sil_ready"], i * UNITS + u + 1)
                            dve.wait_ge(S["alo_ready"], i * UNITS + max(u, 1))
                            v.tensor_tensor(actf[:, u % 2, :], score[:, (u % 2) * 2 + 1, 0:4 * NQ], sil[:, u % 2, :],
                                            ALU.mult).then_inc(S["act_ready"], 1)
                            dve.wait_ge(S["act_ready"], i * UNITS + u + 3)
                            if f == 0:
                                dve.wait_ge(S["down_ready"], i * CHUNKS + J + 1)
                            v.tensor_copy(ahi[:, J % 2, f, :], actf[:, u % 2, :]).then_inc(S["ahi_ready"], 1)
                        if J >= 3:
                            D, j = J - 3, (J - 3) % 4
                            e = 2 * i + D // 4
                            d = D % 2
                            base = i * (2 * CHUNKS) + 2 * D
                            if f == 0:
                                dve.wait_ge(S["coef_ready"], i * CHUNKS + D + 1)
                                gate = route[:NQ, 0, :].rearrange("p (b e) -> p b e", e=E)[:, j * 4:(j + 1) * 4, bass.ds(e, 1)]
                                v.scalar_tensor_tensor(out=coef[:NQ, d, 2, :].unsqueeze(2),
                                                       in0=coef[:NQ, d, 1, :].unsqueeze(2), scalar=1.0 / WSCALE ** 2,
                                                       in1=gate, op0=ALU.mult, op1=ALU.mult).then_inc(S["coef_step"], 1)
                                dve.wait_ge(S["coef_step"], base + 1)
                            last = v.scalar_tensor_tensor(
                                out=term[:NQ, d, f, :], in0=dsb[:NQ, d, f, :], scalar=coef[:NQ, d, 2, f:f + 1],
                                in1=enw[:NQ, bass.ds(e, 1), :].rearrange("p a c -> p (a c)"), op0=ALU.mult, op1=ALU.mult)
                            if f == 3:
                                last.then_inc(S["coef_step"], 1)
                                dve.wait_ge(S["coef_step"], base + 2)
                                v.tensor_tensor(tmp[:NQ, j * 4:(j + 1) * 4, :], tmp[:NQ, j * 4:(j + 1) * 4, :],
                                                term[:NQ, d, :, :], ALU.add).then_inc(S["acc_ready"], 1)
                        if 2 <= J < CHUNKS + 2 and f == 1:
                            dve.wait_ge(S["sq_ready"], i * CHUNKS + J - 1)
                            v.tensor_scalar(coef[:NQ, J % 2, 0, :], ssq[:NQ, J % 2, :], 1.0 / C, RMS_EPS, ALU.mult,
                                            ALU.add).then_inc(S["ms_ready"], 1)
                    if J < CHUNKS and J % 4 < 3:
                        ep, k = J // 4, J % 4
                        weights_lo(1 - ep, k, i * 6 + 3 * (ep + 1) + k + 1)
            dve.wait_ge(S["acc_ready"], E // 2 * CHUNKS + 2)
            rms_norm(lambda b: tmp[:NQ, b, :], outnw)
            for k in range(GLUE):
                dve.wait_ge(S["token_mm"], 2 * GLUE + k + 1)
                xk = xv[:, k * GROUP:(k + 1) * GROUP, :]
                last = v.scalar_tensor_tensor(out=xk, in0=score[:NQ, k, :].rearrange("p (s c) -> p s c", c=C),
                                              scalar=gt[:NQ, 3:4], in1=xk, op0=ALU.mult, op1=ALU.add)
            last.then_inc(S["x_final"], 1)


_INS = ['x', 'ctx_1024', 'g_xattn', 'g_ffn', 'L0_xattn_ln_m_w', 'L0_xattn_ln_m_b', 'L0_xattn_ln_l_w',
        'L0_xattn_ln_l_b', 'L0_xattn_Wq', 'L0_xattn_Wkv', 'L0_xattn_Wout', 'L0_ffn_weight', 'L0_ffn_aux_weight1',
        'L0_ffn_aux_weight2', 'L0_ffn_bias', 'L1_xattn_Wq', 'L1_xattn_Wk', 'L1_xattn_Wv', 'L1_xattn_Wo',
        'L1_xattn_bo', 'L1_ffn_W_in', 'L1_ffn_in_norm_w', 'L1_ffn_Wr', 'L1_ffn_expert_bias', 'L1_ffn_Wg',
        'L1_ffn_Wu', 'L1_ffn_Wd', 'L1_ffn_enorm_w', 'L1_ffn_out_norm_w', 'L1_ffn_W_out']
_OUTS = [((B, NQ, C), 'float32')]


def kernel(**inputs):
    import numpy as _np
    import concourse.bacc as _bacc
    from concourse import mybir as _mybir
    from concourse.bass_utils import run_bass_kernel_spmd as _run

    nc = _bacc.Bacc("TRN2", target_bir_lowering=False, num_devices=1)
    arrays, args = {}, {}
    for name in _INS:
        a = _np.ascontiguousarray(inputs[name])
        arrays[f"in_{name}_dram"] = a
        args[name] = nc.dram_tensor(f"in_{name}_dram", a.shape, _mybir.dt.from_np(a.dtype), kind="ExternalInput").ap()
    for i, (shape, dtype) in enumerate(_OUTS):
        dt = _mybir.dt.from_np(_np.dtype(dtype))
        args["out"] = nc.dram_tensor(f"out_{i}_dram", shape, dt, kind="ExternalOutput").ap()
    flamingo_kernel(nc, args)
    r = _run(nc, [arrays], core_ids=[0])
    return r.results[0]["out_0_dram"]
```
